# Optimizing a Trainium2 kernel written in Bass

```python
import numpy as np
import jax
import jax.numpy as jnp

def _softmax(x, axis=-1):
    return jax.nn.softmax(x, axis=axis)

def _gelu(x):
    return jax.nn.gelu(x, approximate=True)

def _silu(x):
    return jax.nn.silu(x)

def _sigmoid(x):
    return jax.nn.sigmoid(x)

def _layernorm(x, axis=-1, eps=1e-05):
    m = jnp.mean(x, axis=axis, keepdims=True)
    v = jnp.var(x, axis=axis, keepdims=True)
    return (x - m) / jnp.sqrt(v + eps)

def _scatter_add(tgt, idx, src, axis=0):
    return tgt.at[idx].add(src)

def _segment_sum(src, seg, n):
    return jax.ops.segment_sum(src, seg, n)
kernel_name = 'mk_xattn_ffn_d1_seqx_r4_d154cd'

def setup_inputs(seed: int=0):
    np.random.seed(seed)
    _w = jnp.asarray

    def _rec_inputs():
        import jax
        import jax.numpy as jnp
        _rk = jax.random.key(seed)
        x = -0.0002928 + 1 * jax.random.normal(jax.random.fold_in(_rk, 1), (4, 1024, 256), jnp.float32)
        _lenS = 1024 - jax.random.randint(jax.random.fold_in(_rk, 7), (4,), 0, max(1, 1024 // 4) + 1, jnp.int32)
        _lenS2 = 154 - jax.random.randint(jax.random.fold_in(_rk, 8), (4,), 0, max(1, 154 // 4) + 1, jnp.int32)
        _ctx_1024P = jax.random.normal(jax.random.fold_in(_rk, 11), (4, 16, 256), jnp.float32)
        _ctx_1024c = jax.random.dirichlet(jax.random.fold_in(_rk, 511), 0.3 * jnp.ones((16,), jnp.float32), (4, 154))
        _ctx_1024t = jnp.einsum('bsk,bkd->bsd', _ctx_1024c, _ctx_1024P)
        _ctx_1024t = _ctx_1024t * jax.lax.rsqrt(jnp.mean(jnp.square(_ctx_1024t)) + 1e-12) * 0.953939
        ctx_1024 = -1.39393e-06 + 0.999914 * (_ctx_1024t + 0.3 * jax.random.normal(jax.random.fold_in(_rk, 611), (4, 154, 256), jnp.float32))
        _validS = jnp.arange(1024)[None, :] < _lenS[:, None]
        _validS2 = jnp.arange(154)[None, :] < _lenS2[:, None]
        _causal = jnp.tril(jnp.ones((1024, 1024), dtype=bool))
        mask_1x1xSxS2_bk0 = jnp.logical_not(jnp.broadcast_to(_validS2[0:1, None, None, :], (1, 1, 1024, 154)))
        return (x, ctx_1024, mask_1x1xSxS2_bk0)
    x, ctx_1024, mask_1x1xSxS2_bk0 = _rec_inputs()

    def _L0_xattn_setup():
        import jax, jax.numpy as jnp
        import numpy as np
        import math
        D_MODEL = 256
        N_HEADS = 16
        D_K = D_MODEL // N_HEADS
        B, S = (2, 512)
        key = jax.random.key(seed)
        ks = jax.random.split(key, 8)
        sc = 1.0 / math.sqrt(D_MODEL)
        Q = jax.random.normal(ks[0], (B, S, D_MODEL), jnp.float32)
        K = jax.random.normal(ks[1], (B, S, D_MODEL), jnp.float32)
        V = jax.random.normal(ks[2], (B, S, D_MODEL), jnp.float32)
        mask = jnp.tril(jnp.ones((S, S), dtype=bool))[None, None, :, :]
        Wq = jax.random.normal(ks[3], (D_MODEL, D_MODEL), jnp.float32) * sc
        Wk = jax.random.normal(ks[4], (D_MODEL, D_MODEL), jnp.float32) * sc
        Wv = jax.random.normal(ks[5], (D_MODEL, D_MODEL), jnp.float32) * sc
        Wo = jax.random.normal(ks[6], (D_MODEL, D_MODEL), jnp.float32) * sc
        bo = jnp.zeros((D_MODEL,), jnp.float32)
        return {'Q': Q, 'K': K, 'V': V, 'mask': mask, 'Wq': Wq, 'Wk': Wk, 'Wv': Wv, 'Wo': Wo, 'bo': bo}
    _L0_xattn_all = _L0_xattn_setup()
    _L0_xattn_in = {k: v for k, v in _L0_xattn_all.items() if k in ('Wq', 'Wk', 'Wv', 'Wo', 'bo')}
    del _L0_xattn_all

    def _L0_ffn_setup():
        import jax, jax.numpy as jnp
        import numpy as np
        FP8_MAX = 448.0
        SCALE = 1.0
        _FP8_DTYPE = getattr(jnp, 'float8_e4m3fn', jnp.float16)

        def quantize_e4m3(t, scale):
            return jnp.clip(t / scale, -FP8_MAX, FP8_MAX).astype(_FP8_DTYPE)
        key = jax.random.key(seed)
        kx, kw = jax.random.split(key)
        B, N, C, F = (8, 1024, 256, 256)
        x = jax.random.normal(kx, (B, N, C), dtype=jnp.float32)
        weight = jax.random.normal(kw, (F, C), dtype=jnp.float32) * 0.02
        bias = jnp.zeros((F,), dtype=jnp.float32)
        return {'x': x, 'weight': weight, 'bias': bias}
    _L0_ffn_all = _L0_ffn_setup()
    _L0_ffn_in = {k: v for k, v in _L0_ffn_all.items() if k in ('weight', 'bias')}
    del _L0_ffn_all
    return {'x': x, 'ctx_1024': ctx_1024, 'mask_1x1xSxS2_bk0': mask_1x1xSxS2_bk0, 'L0_xattn_Wq': _L0_xattn_in['Wq'], 'L0_xattn_Wk': _L0_xattn_in['Wk'], 'L0_xattn_Wv': _L0_xattn_in['Wv'], 'L0_xattn_Wo': _L0_xattn_in['Wo'], 'L0_xattn_bo': _L0_xattn_in['bo'], 'L0_ffn_weight': _L0_ffn_in['weight'], 'L0_ffn_bias': _L0_ffn_in['bias']}

def reference(x, ctx_1024, mask_1x1xSxS2_bk0, L0_xattn_Wq, L0_xattn_Wk, L0_xattn_Wv, L0_xattn_Wo, L0_xattn_bo, L0_ffn_weight, L0_ffn_bias):
    import jax
    import jax.numpy as jnp

    def _L0_xattn_ref(Q, K, V, mask, Wq, Wk, Wv, Wo, bo):
        import jax, jax.numpy as jnp
        import numpy as np
        import math
        D_MODEL = 256
        N_HEADS = 16
        D_K = D_MODEL // N_HEADS
        B, S = (2, 512)
        b, s, d = Q.shape

        def split(x):
            return x.reshape(b, -1, N_HEADS, D_K).transpose(0, 2, 1, 3)
        q = split(Q @ Wq.T)
        k = split(K @ Wk.T)
        v = split(V @ Wv.T)
        scores = jnp.einsum('bhsd,bhtd->bhst', q, k) / math.sqrt(D_K)
        scores = jnp.where(mask, scores, jnp.float32(-1000000000.0))
        attn = jax.nn.softmax(scores, axis=-1)
        out = jnp.einsum('bhst,bhtd->bhsd', attn, v)
        out = out.transpose(0, 2, 1, 3).reshape(b, s, d)
        return out @ Wo.T + bo

    def _L0_ffn_ref(x, weight, bias):
        import jax, jax.numpy as jnp
        import numpy as np
        FP8_MAX = 448.0
        SCALE = 1.0
        _FP8_DTYPE = getattr(jnp, 'float8_e4m3fn', jnp.float16)

        def quantize_e4m3(t, scale):
            return jnp.clip(t / scale, -FP8_MAX, FP8_MAX).astype(_FP8_DTYPE)
        B, N, C = x.shape
        x2d = x.reshape(B * N, C)
        x_mat = quantize_e4m3(x2d, SCALE).astype(jnp.float16)
        w_mat = quantize_e4m3(weight, SCALE).astype(jnp.float16)
        out2d = (x_mat @ w_mat.T).astype(jnp.float32) * (SCALE * SCALE)
        out2d = out2d + bias
        return out2d.reshape(B, N, -1)
    x = x + _L0_xattn_ref(_layernorm(x, axis=-1), ctx_1024, ctx_1024, mask_1x1xSxS2_bk0, L0_xattn_Wq, L0_xattn_Wk, L0_xattn_Wv, L0_xattn_Wo, L0_xattn_bo)
    x = x + _L0_ffn_ref(_layernorm(x, axis=-1), L0_ffn_weight, L0_ffn_bias)
    return x

_drawn_inputs = setup_inputs


def setup_inputs(seed=0):
    import zlib

    import numpy as np

    out = dict(_drawn_inputs(seed))
    spreads = {'L0_xattn_bo': (0.0, 0.1), 'L0_ffn_bias': (0.0, 0.1)}
    factors = {}
    for name, (base, spread) in spreads.items():
        noise = np.random.default_rng([zlib.crc32(name.encode()), seed]).standard_normal(out[name].shape)
        drawn = base * np.exp(spread * noise) if base else spread * noise
        out[name] = jnp.asarray(drawn.astype(out[name].dtype))
    for name, factor in factors.items():
        out[name] = (out[name] * factor).astype(out[name].dtype)
    return out
```

```python
from contextlib import ExitStack

import concourse.bass as bass
from concourse import mybir

ALU = mybir.AluOpType
ACT = mybir.ActivationFunctionType
X = mybir.AxisListType.X
XY = mybir.AxisListType.XY
F32 = mybir.dt.float32
F16 = mybir.dt.float16
BF16 = mybir.dt.bfloat16
F8 = mybir.dt.float8e4
I32 = mybir.dt.int32
U8 = mybir.dt.uint8
RMAX = bass.bass_isa.ReduceOp.max

P = 128
H = 16
DK = 16
NP = H // 2
G = H // 4
T = 4
R = P * T
LW = 32
KR = 97 + H
KM = 97
NEG = -60000.0
EPS = 1e-5
RS = 64.0
CH = 5


def at(k, per, plus=0):
    return k[0] * (2 * per) + (k[1] * per + plus)


def ahead(k, d):
    n = k[1] + d
    return (k[0] + n // 2, n % 2)


def first(k, d=0):
    return isinstance(k[0], int) and 2 * k[0] + k[1] - d < 0


def xattn_ffn(nc, x, ctx, mask, wq, wk, wv, wo, bo, wf, bf, out):
    B, S, D = x.shape
    SK = ctx.shape[1]
    C = D // P
    L = SK - P
    KP = P + LW
    CT = SK // 2
    NB = B * S // R
    VB = H * LW + G * P
    ST = S // R
    assert D == C * P and D == H * DK and 0 < L <= LW and ST == 2 and CT * 2 == SK and NB == 2 * B

    x_rows = x.rearrange("b (s p t) c -> (b s) p t c", p=P, t=T)
    out_rows = out.rearrange("b (s p t) c -> (b s) p t c", p=P, t=T)
    mask_rows = mask.rearrange("a h (s p t) k -> p s t (a h k)", p=P, t=T)

    q_dram = nc.dram_tensor("q_dram", (2, 2, D, R), F16, kind="Internal").ap()
    k_dram = nc.dram_tensor("k_dram", (2, D, B * KP), F16, kind="Internal").ap()
    s_dram = nc.dram_tensor("s_dram", (H * R,), F32, kind="Internal").ap()
    r_dram = nc.dram_tensor("r_dram", (2, H * R), F16, kind="Internal").ap()

    with ExitStack() as stack:
        def sb(name, shape, dt):
            return stack.enter_context(nc.sbuf_tensor(name, shape, dt))

        def sem(name):
            return stack.enter_context(nc.semaphore(name))

        ident = sb("ident", [P, P], F32)
        ident16 = sb("ident16", [P, P], F16)
        identb = sb("identb", [P, P], BF16)
        ident8 = sb("ident8", [P, P], F8)
        w_t = sb("w_t", [P, 4, C, D], F32)
        wf_t = sb("wf_t", [P, C, D], BF16)
        bo_all = sb("bo_all", [P, D], F32)
        bf_all = sb("bf_all", [P, D], F32)
        half = sb("half", [P, T], F32)
        k_hi = sb("k_hi", [P, C, B, KP], F16)
        k_lo = sb("k_lo", [P, C, B, KP], F16)
        k_all = sb("k_all", [KR, NP, 2, B, KP], F16)
        k_max = sb("k_max", [KR, NP, 2, KP], F16)
        k_now = sb("k_now", [KR, NP, 2, KP], F16)
        v_all = sb("v_all", [P, B, VB], F32)
        v_now = sb("v_now", [P, VB], F32)
        mask_in = sb("mask_in", [P, ST * T, SK], U8)
        row_keep = sb("row_keep", [P, ST * T], F32)
        col_part = sb("col_part", [P, SK], F32)
        col_keep = sb("col_keep", [P, SK], F32)
        mask_own = sb("mask_own", [P, ST * T, KP], F16)
        own_part = sb("own_part", [P, 1], F32)
        own_any = sb("own_any", [P, 1], F32)
        own_flag = sb("own_flag", [1, 1], I32)
        neg_row = sb("neg_row", [1, KP], F16)
        x_a = sb("x_a", [P, 2, T, D], F32)
        st_a = sb("st_a", [P, T, 6], F32)
        mv_a = sb("mv_a", [P, T, 2], F32)
        ve_a = sb("ve_a", [P, 2, T], F32)
        rs_a = sb("rs_a", [P, 3, T], F32)
        xn = sb("xn", [P, T, D], F32)
        xn_t = sb("xn_t", [P, C, R], F32)
        q_hi = sb("q_hi", [P, C, R], F16)
        q_lo = sb("q_lo", [P, C, R], F16)
        q_st = sb("q_st", [KR, 2, NP, R], F16)
        m_neg = sb("m_neg", [P, T, H], F32)
        m_t = sb("m_t", [H, R], F16)
        p_t = sb("p_t", [P, 2, CH, R], F32)
        o_t = sb("o_t", [P, 2, G, R], F32)
        sums = sb("sums", [P, R * H // P], F32)
        rsum = sb("rsum", [P, R * H // P], F32)
        rs_16 = sb("rs_16", [P, 2, R * H // P], F16)
        rs_row = sb("rs_row", [2 * H, R], F16)
        spread = sb("spread", [2 * H, C, P], F16)
        a_raw = sb("a_raw", [P, C, R], F32)
        a_t = sb("a_t", [P, C, R], F32)
        x_c = sb("x_c", [P, 2, T, D], F32)
        x_bo = sb("x_bo", [P, T, D], F32)
        x1 = sb("x1", [P, T, D], F32)
        st_c = sb("st_c", [P, T, 6], F32)
        mv_c = sb("mv_c", [P, T, 2], F32)
        ve_c = sb("ve_c", [P, T], F32)
        rs_c = sb("rs_c", [P, T], F32)
        xq = sb("xq", [P, T, D], F8)
        xq_t = sb("xq_t", [P, C, R], BF16)
        x1_bf = sb("x1_bf", [P, T, D], F32)
        ff = sb("ff", [P, T, D], F16)
        y = sb("y", [P, 2, T, D], F32)

        raw = p_t[:].rearrange("p a c r -> p (a c r)")
        NW = C * D
        w_raw = raw[:, 0:5 * NW].rearrange("p (i o n) -> p i o n", i=5, o=C)
        wf_small = raw[:, 5 * NW:6 * NW].rearrange("p (o n) -> p o n", o=C)
        wf_big = raw[:, 6 * NW:7 * NW].rearrange("p (o n) -> p o n", o=C)
        wf_8 = raw[:, 7 * NW:7 * NW + NW // 2].bitcast(F8).rearrange("p (i o n) -> p i o n", i=2, o=C)
        wf_q = raw[:, 8 * NW:8 * NW + NW // 2].bitcast(BF16).rearrange("p (o n) -> p o n", o=C)
        ctx_in = y[0:CT].rearrange("p a t c -> p (a t) c")
        k_ones = x_c[0:H].rearrange("p a t c -> p (a t c)").bitcast(F16)[:, 0:H * KP].rearrange(
            "p (h k) -> p h k", k=KP)
        spare = o_t[:].rearrange("p a g r -> p (a g r)")
        ctx_t = spare[:, 0:C * B * SK].rearrange("p (c k) -> p c k", c=C)
        keep = spare[:, C * B * SK:C * B * SK + ST * T * SK].rearrange("p (t k) -> p t k", k=SK)

        ps = stack.enter_context(nc.psum_tensor("ps", [P, 8, 512], F32))
        wf_ps = ps[:, 0, 0:C * D // 2].bitcast(BF16)
        SC, OB, MX, GP = 0, 3, 4, 6

        ctx_in_s = sem("ctx_in_s")
        w_in = [sem(f"w_in{i}") for i in range(5)]
        mask_in_s = sem("mask_in_s")
        bias_in = sem("bias_in")
        x_a_in = [sem("x_a_in0"), sem("x_a_in1")]
        x_c_in = [sem("x_c_in0"), sem("x_c_in1")]
        pool_const = sem("pool_const")
        dve_const = sem("dve_const")
        zeroed = sem("zeroed")
        q_ones = sem("q_ones")
        pro_pe = sem("pro_pe")
        pro_act = sem("pro_act")
        k_split = sem("k_split")
        v_built = sem("v_built")
        mask_dve = sem("mask_dve")
        mask_pool = sem("mask_pool")
        wf_dve = sem("wf_dve")
        k_sent = sem("k_sent")
        k_built = sem("k_built")
        kmax_in = sem("kmax_in")
        know_in = sem("know_in")
        vnow_in = sem("vnow_in")
        lna_dve = sem("lna_dve")
        lna_stats = sem("lna_stats")
        lna_pool = sem("lna_pool")
        xn_ready = sem("xn_ready")
        xt_done = sem("xt_done")
        xt_out = sem("xt_out")
        q_done = sem("q_done")
        qhi_out = sem("qhi_out")
        qlo_out = sem("qlo_out")
        q_sent = sem("q_sent")
        q_stacked = [sem("q_stacked0"), sem("q_stacked1")]
        max_done = sem("max_done")
        max_red = sem("max_red")
        mt_done = sem("mt_done")
        mt_out = sem("mt_out")
        m_stacked = [sem("m_stacked0"), sem("m_stacked1")]
        sc_done = sem("sc_done")
        exp_done = sem("exp_done")
        pv_done = sem("pv_done")
        ot_out = sem("ot_out")
        a_in = [sem("a_in0"), sem("a_in1")]
        sums_sent = sem("sums_sent")
        sums_in = sem("sums_in")
        recip = sem("recip")
        rs_split = sem("rs_split")
        rs_sent = sem("rs_sent")
        rsrow_in = sem("rsrow_in")
        rs_spread = sem("rs_spread")
        at_ready = sem("at_ready")
        xbo_ready = sem("xbo_ready")
        wo_done = sem("wo_done")
        x1_ready = sem("x1_ready")
        lnc_dve = sem("lnc_dve")
        lnc_stats = sem("lnc_stats")
        lnc_rstd = sem("lnc_rstd")
        xq_ready = sem("xq_ready")
        xqt_done = sem("xqt_done")
        xqt_out = sem("xqt_out")
        x1bf_ready = sem("x1bf_ready")
        ff_done = sem("ff_done")
        ff_out = sem("ff_out")
        y_ready = sem("y_ready")
        stored = [sem("stored0"), sem("stored1")]

        past_sp, past_pool, past_dve, past_pe = (sem(f"past_{e}") for e in ("sp", "pool", "dve", "pe"))

        LAST = (B - 1, 1)

        block = stack.enter_context(nc.Block())

        @block.sync
        def _(sp):
            def load_x_a(k):
                if not first(k, 2):
                    sp.wait_ge(xn_ready, at(k, 1, -1))
                sp.sem_inc(past_sp, 1)
                sp.dma_start(x_a[:, k[1]], x_rows[bass.ds(at(k, 1), 1)].rearrange("s p t c -> p (s t) c")
                             ).then_inc(x_a_in[k[1]], 16)

            def load_x_c(k):
                if not first(k, 2):
                    sp.wait_ge(xbo_ready, at(k, 1, -1))
                sp.sem_inc(past_sp, 1)
                sp.dma_start(x_c[:, k[1]], x_rows[bass.ds(at(k, 1), 1)].rearrange("s p t c -> p (s t) c")
                             ).then_inc(x_c_in[k[1]], 16)

            def stack_q(k):
                sp.wait_ge(qhi_out, at(k, C, C))
                sp.wait_ge(qlo_out, at(k, C, C))
                for n, part in enumerate((q_hi, q_lo)):
                    sp.dma_start(q_dram[k[1], n].rearrange("(c p) r -> p c r", p=P), part[:]).then_inc(q_sent, 16)
                sp.wait_ge(q_sent, at(k, 32, 32))
                if not first(k, 2):
                    sp.sem_inc(past_sp, 1)
                    sp.wait_ge(sc_done, at(k, G * CH, -G * CH))
                for n, part in enumerate((0, 0, 1)):
                    sp.dma_start(q_st[32 * n:32 * n + 32, k[1]],
                                 q_dram[k[1], part].rearrange("(p d) r -> d p r", d=32)
                                 ).then_inc(q_stacked[k[1]], 16)

            def stack_m(k):
                sp.wait_ge(mt_out, at(k, 1, 1))
                sp.dma_start(q_st[KM:KR, k[1]], m_t[:, None, :].to_broadcast([H, NP, R])).then_inc(m_stacked[k[1]], 16)

            def outputs(k, g):
                sp.wait_ge(ot_out, at(k, G, g + 1))
                if g == 0 and not first(k, 1):
                    sp.sem_inc(past_sp, 1)
                    sp.wait_ge(at_ready, at(k, C))
                sp.dma_start(a_raw[64 * (g % 2):64 * (g % 2) + 64, g // 2], o_t[0:P:2, k[1], g]
                             ).then_inc(a_in[k[1]], 16)

            def gather_sums(k):
                sp.wait_ge(ot_out, at(k, G, G))
                sp.dma_start(s_dram.rearrange("(g i r) -> i g r", i=4, r=R), o_t[1:P:32, k[1]]
                             ).then_inc(sums_sent, 16)
                sp.wait_ge(sums_sent, at(k, 16, 16))
                if not first(k, 1):
                    sp.sem_inc(past_sp, 1)
                    sp.wait_ge(recip, at(k, 1))
                sp.dma_start(sums[:, :], s_dram.rearrange("(p w) -> p w", p=P)).then_inc(sums_in, 16)

            def send_reciprocals(k):
                sp.wait_ge(rs_split, at(k, 2, 2))
                sp.dma_start(r_dram.rearrange("i (p w) -> p i w", p=P), rs_16[:]).then_inc(rs_sent, 16)
                sp.wait_ge(rs_sent, at(k, 16, 16))
                if not first(k, 1):
                    sp.sem_inc(past_sp, 1)
                    sp.wait_ge(rs_spread, at(k, C))
                sp.dma_start(rs_row[:, :], r_dram.rearrange("i (h r) -> (i h) r", r=R)).then_inc(rsrow_in, 16)

            def keys_of(b):
                return k_all[:].rearrange("r p s b k -> r (p s) (b k)")[:, :, bass.ds(b * KP, KP)]

            def k_max_for(b, seen):
                sp.wait_ge(max_done, seen)
                sp.sem_inc(past_sp, 1)
                sp.dma_start(k_max[:].rearrange("r p s k -> r (p s) k"), keys_of(b)).then_inc(kmax_in, 16)

            def k_v_now_for(b, scored, summed):
                sp.wait_ge(sc_done, scored)
                sp.sem_inc(past_sp, 1)
                sp.dma_start(k_now[:].rearrange("r p s k -> r (p s) k"), keys_of(b)).then_inc(know_in, 16)
                sp.wait_ge(pv_done, summed)
                sp.sem_inc(past_sp, 1)
                sp.dma_start(v_now[:, :], v_all[:].rearrange("p b n -> p (b n)")[:, bass.ds(b * VB, VB)]
                             ).then_inc(vnow_in, 16)

            def store(k):
                sp.wait_ge(y_ready, at(k, 1, 1))
                sp.sem_inc(past_sp, 1)
                sp.dma_start(out_rows[bass.ds(at(k, 1), 1)].rearrange("s p t c -> p (s t) c"), y[:, k[1]]
                             ).then_inc(stored[k[1]], 16)

            for i, w in ((0, wq), (4, wf)):
                sp.dma_start(w_raw[:, i], w.rearrange("(o p) n -> p o n", p=P)).then_inc(w_in[i], 16)
            load_x_a((0, 0))
            sp.dma_start(mask_in[:, :, :].rearrange("p (s t) k -> p s t k", s=ST), mask_rows
                         ).then_inc(mask_in_s, 16)
            load_x_a((0, 1))
            sp.dma_start(bo_all[:, :], bass.AP(bo.tensor, 0, [[0, P], [1, D]])).then_inc(bias_in, 16)
            sp.dma_start(bf_all[:, :], bass.AP(bf.tensor, 0, [[0, P], [1, D]])).then_inc(bias_in, 16)

            sp.wait_ge(q_ones, 1)
            sp.wait_ge(zeroed, 2)
            sp.wait_ge(k_split, 2 * 2 * C)
            for n, part in enumerate((k_hi, k_lo)):
                sp.dma_start(k_dram[n].rearrange("(c p) k -> p c k", p=P),
                             part[:].rearrange("p c b k -> p c (b k)")).then_inc(k_sent, 16)
            for b in range(B):
                sp.dma_start(k_all[KM:KR, :, :, b].rearrange("r p s k -> r (p s) k"), k_ones).then_inc(k_built, 16)
            sp.wait_ge(k_sent, 32)
            for s in range(2):
                for n, part in enumerate((0, 1, 0)):
                    row = 32 * n + DK * s
                    sp.dma_start(k_all[row:row + DK, :, s].rearrange("r p b k -> r p (b k)"),
                                 k_dram[part].rearrange("(p s d) k -> s d p k", s=2, d=DK)[s]).then_inc(k_built, 16)
            sp.wait_ge(mask_dve, 6)
            src = bass.AP(neg_row[:].tensor, 0, [[KP, 1], [0, B * NP * 2], [1, KP]])
            sp.dma_start(k_all[KM - 1:KM].rearrange("r p s b k -> r (p s b) k"), src).then_inc(k_built, 16)
            sp.wait_ge(k_built, 16 * (B + 2 * 3 + 1))
            stack_q((0, 0))
            sp.dma_start(k_max[:].rearrange("r p s k -> r (p s) k"), keys_of(0)).then_inc(kmax_in, 16)
            sp.dma_start(k_now[:].rearrange("r p s k -> r (p s) k"), keys_of(0)).then_inc(know_in, 16)
            sp.wait_ge(v_built, 1)
            sp.dma_start(v_now[:, :], v_all[:, 0]).then_inc(vnow_in, 16)
            stack_m((0, 0))

            def step(k, more=2, back=True, new_batch=None):
                if more > 1:
                    load_x_a(ahead(k, 2))
                if more:
                    stack_q(ahead(k, 1))
                    if new_batch is not None:
                        k_max_for(new_batch, at(ahead(k, 1), T * NP))
                if back:
                    send_reciprocals(ahead(k, -1))
                load_x_c(k)
                for g in range(G):
                    outputs(k, g)
                gather_sums(k)
                if more:
                    stack_m(ahead(k, 1))
                    if new_batch is not None:
                        k_v_now_for(new_batch, at(k, G * CH, G * CH), at(k, G, G))
                if back:
                    store(ahead(k, -1))

            step((0, 0), back=False)
            step((0, 1), new_batch=1)
            with sp.Fori(1, B - 1) as h:
                step((h, 0))
                step((h, 1), new_batch=h + 1)
            step((B - 1, 0), more=1)
            step(LAST, more=0)
            send_reciprocals(LAST)
            store(LAST)
            sp.wait_ge(stored[0], 16 * B)
            sp.wait_ge(stored[1], 16 * B)

        @block.gpsimd
        def _(pool):
            nc.gpsimd.memset(ident[:, :], 0.0).then_inc(pool_const, 1)
            nc.gpsimd.memset(half[:, :], -0.5).then_inc(pool_const, 1)
            pool.wait_ge(pool_const, 2)
            nc.gpsimd.affine_select(out=ident[:, :], in_=ident[:, :], compare_op=ALU.not_equal, fill=1.0,
                                    base=0, pattern=[[-1, P]], channel_multiplier=1).then_inc(pool_const, 1)
            nc.gpsimd.memset(k_all[:].rearrange("r p s b k -> r (p s b k)").bitcast(F32), 0.0
                             ).then_inc(zeroed, 1)
            nc.gpsimd.memset(k_ones, 0.0).then_inc(pool_const, 1)
            pool.wait_ge(pool_const, 4)
            nc.gpsimd.affine_select(out=k_ones, in_=k_ones, compare_op=ALU.not_equal, fill=1.0, base=0,
                                    pattern=[[-1, H], [0, KP]], channel_multiplier=1).then_inc(zeroed, 1)
            nc.gpsimd.memset(spread[:], 0.0).then_inc(pool_const, 1)
            for part in range(2):
                pool.wait_ge(pool_const, 5 + part)
                to = spread[:].rearrange("p c (h d) -> p c h d", d=DK)
                nc.gpsimd.affine_select(out=to, in_=to, compare_op=ALU.not_equal, fill=1.0 / RS, base=-H * part,
                                        pattern=[[-8, C], [-1, 8], [0, DK]], channel_multiplier=1
                                        ).then_inc(pool_const, 1)

            def ln_a(k):
                pool.wait_ge(lna_stats, at(k, 1, 1))
                nc.gpsimd.tensor_tensor(rs_a[:, 0], ve_a[:, 0], half[:, :], ALU.pow).then_inc(lna_pool, 1)
                pool.wait_ge(lna_pool, at(k, 3, 1))
                pool.wait_ge(mask_dve, 2)
                nc.gpsimd.tensor_tensor(rs_a[:, 1], rs_a[:, 0], row_keep[:, T * k[1]:T * k[1] + T], ALU.mult
                                        ).then_inc(lna_pool, 1)
                pool.wait_ge(lna_pool, at(k, 3, 2))
                nc.gpsimd.tensor_tensor(rs_a[:, 2], rs_a[:, 1], ve_a[:, 1], ALU.mult).then_inc(lna_pool, 1)
                pool.wait_ge(lna_pool, at(k, 3, 3))
                if not first(k, 1):
                    pool.wait_ge(xt_done, at(k, C))
                pool.sem_inc(past_pool, 1)
                for t in range(T):
                    last = nc.gpsimd.tensor_scalar(xn[:, t], x_a[:, k[1], t], rs_a[:, 1, t:t + 1],
                                                   rs_a[:, 2, t:t + 1], ALU.mult, ALU.add)
                last.then_inc(xn_ready, 1)

            def residual(k):
                pool.wait_ge(bias_in, 32)
                pool.wait_ge(x_c_in[k[1]], at((k[0], 0), 8, 16))
                if not first(k, 1):
                    pool.wait_ge(x1_ready, at(k, C))
                nc.gpsimd.tensor_tensor(x_bo[:], x_c[:, k[1]], bo_all[:, None, :].to_broadcast([P, T, D]),
                                        ALU.add).then_inc(xbo_ready, 1)

            def ln_c(k):
                pool.wait_ge(lnc_stats, at(k, 1, 1))
                nc.gpsimd.tensor_tensor(rs_c[:, :], ve_c[:, :], half[:, :], ALU.pow).then_inc(lnc_rstd, 1)
                pool.wait_ge(x1_ready, at(k, C, C))
                nc.gpsimd.tensor_tensor(x1_bf[:], x1[:], bf_all[:, None, :].to_broadcast([P, T, D]), ALU.add
                                        ).then_inc(x1bf_ready, 1)

            def finish(k):
                pool.wait_ge(x1bf_ready, at(k, 1, 1))
                pool.wait_ge(ff_out, at(k, C, C))
                if not first(k, 2):
                    pool.wait_ge(stored[k[1]], at((k[0], 0), 8))
                nc.gpsimd.tensor_tensor(y[:, k[1]], x1_bf[:], ff[:], ALU.add).then_inc(y_ready, 1)

            ln_a((0, 0))
            pool.wait_ge(mask_dve, 3)
            nc.gpsimd.partition_all_reduce(col_keep[:, :], col_part[:, :], P, RMAX).then_inc(mask_pool, 1)
            pool.wait_ge(mask_dve, 5)
            nc.gpsimd.partition_all_reduce(own_any[:, :], own_part[:, :], P, RMAX).then_inc(mask_pool, 1)
            ln_a((0, 1))

            def step(k, more=2, back=True):
                if more > 1:
                    ln_a(ahead(k, 2))
                residual(k)
                if back:
                    ln_c(ahead(k, -1))
                    finish(ahead(k, -1))

            step((0, 0), back=False)
            step((0, 1))
            with pool.Fori(1, B - 1) as h:
                step((h, 0))
                step((h, 1))
            step((B - 1, 0), more=1)
            step(LAST, more=0)
            ln_c(LAST)
            finish(LAST)

        @block.scalar
        def _(act):
            act.dma_start(ctx_in, ctx.rearrange("b (u r) c -> r (b u) c", u=2)).then_inc(ctx_in_s, 16)
            for i, w in ((1, wk), (2, wv), (3, wo)):
                act.dma_start(w_raw[:, i], w.rearrange("(o p) n -> p o n", p=P)).then_inc(w_in[i], 16)

            def evacuate(n, dst, src):
                act.wait_ge(pro_pe, n)
                nc.scalar.activation(dst, src, ACT.Copy).then_inc(pro_act, 1)

            for i in range(4):
                evacuate(i + 1, w_t[:, i].rearrange("p c n -> p (c n)"), ps[:, i])
            for n in range(4):
                c, s = n // 2, n % 2
                evacuate(5 + n, ctx_t[:, c, s * 2 * SK:(s + 1) * 2 * SK], ps[:, 4 + n, 0:2 * SK])

            evacuate(15, wf_t[:].rearrange("p c n -> p (c n)"), wf_ps)

            def x_transposed(k):
                for c in range(C):
                    act.wait_ge(xt_done, at(k, C, c + 1))
                    if not first(k, 1) and c == 0:
                        act.wait_ge(q_done, at(k, C))
                    nc.scalar.activation(xn_t[:, c], ps[:, GP + 1 - c], ACT.Copy).then_inc(xt_out, 1)

            def q_high(k):
                for c in range(C):
                    act.wait_ge(q_done, at(k, C, c + 1))
                    if not first(k, 1) and c == 0:
                        act.wait_ge(q_sent, at(k, 32))
                    nc.scalar.activation(q_hi[:, c], ps[:, GP + 1 - c], ACT.Copy).then_inc(qhi_out, 1)

            def max_transposed(k):
                act.wait_ge(mt_done, at(k, 1, 1))
                if not first(k, 1):
                    j = ahead(k, -1)
                    act.wait_ge(m_stacked[j[1]], at((j[0], 0), 8, 16))
                nc.scalar.activation(m_t[:, :], ps[0:H, GP], ACT.Copy).then_inc(mt_out, 1)

            def exps(k, g):
                if not first(k, 1) or g >= 2:
                    act.wait_ge(pv_done, at(k, G, g - 1))
                for c in range(CH):
                    n = g * CH + c
                    act.wait_ge(sc_done, at(k, G * CH, n + 1))
                    nc.scalar.activation(p_t[:, g % 2, c], ps[:, SC + n % 3], ACT.Exp, scale=DK ** -0.5
                                         ).then_inc(exp_done, 1)

            def heads_out(k, g):
                act.wait_ge(pv_done, at(k, G, g + 1))
                if g == 0 and not first(k, 2):
                    act.wait_ge(a_in[k[1]], at((k[0], 0), 8 * G))
                    act.wait_ge(sums_sent, at(k, 16, -16))
                nc.scalar.activation(o_t[:, k[1], g], ps[:, OB], ACT.Copy).then_inc(ot_out, 1)

            def quantised_transposed(k):
                for c in range(C):
                    act.wait_ge(xqt_done, at(k, C, c + 1))
                    if not first(k, 1) and c == 0:
                        act.wait_ge(ff_done, at(k, C))
                    nc.scalar.activation(xq_t[:, c], ps[:, GP + c], ACT.Copy).then_inc(xqt_out, 1)

            def layer_out(k):
                for u in range(C):
                    act.wait_ge(ff_done, at(k, C, u + 1))
                    if not first(k, 1) and u == 0:
                        act.wait_ge(y_ready, at(k, 1))
                    nc.scalar.activation(ff[:, 2 * u:2 * u + 2].rearrange("p t c -> p (t c)"), ps[:, GP + u],
                                         ACT.Copy).then_inc(ff_out, 1)

            x_transposed((0, 0))
            q_high((0, 0))
            x_transposed((0, 1))
            max_transposed((0, 0))
            q_high((0, 1))

            def step(k, more=2, back=True):
                j = ahead(k, -1)
                exps(k, 0)
                exps(k, 1)
                heads_out(k, 0)
                exps(k, 2)
                heads_out(k, 1)
                exps(k, 3)
                heads_out(k, 2)
                heads_out(k, 3)
                if more > 1:
                    x_transposed(ahead(k, 2))
                if back:
                    quantised_transposed(j)
                if more > 0:
                    max_transposed(ahead(k, 1))
                if more > 1:
                    q_high(ahead(k, 2))
                if back:
                    layer_out(j)

            step((0, 0), back=False)
            step((0, 1))
            with act.Fori(1, B - 1) as h:
                step((h, 0))
                step((h, 1))
            step((B - 1, 0), more=1)
            step(LAST, more=0)
            quantised_transposed(LAST)
            layer_out(LAST)

        @block.vector
        def _(dve):
            def ln_stats(k, src, stats, mv, done):
                for t in range(T):
                    nc.vector.bn_stats(stats[:, t], src[:, t]).then_inc(done, 1)
                for t in range(T):
                    dve.wait_ge(done, at(k, 2 * T, t + 1))
                    dve.sem_inc(past_dve, 1)
                    nc.vector.bn_aggr(mv[:, t], stats[:, t]).then_inc(done, 1)
                dve.wait_ge(done, at(k, 2 * T, 2 * T))

            def ln_a(k):
                dve.wait_ge(x_a_in[k[1]], at((k[0], 0), 8, 16))
                ln_stats(k, x_a[:, k[1]], st_a, mv_a, lna_dve)
                if not first(k, 1):
                    dve.wait_ge(lna_pool, at(k, 3))
                nc.vector.tensor_scalar(ve_a[:, 0], mv_a[:, :, 1], EPS, None, ALU.add)
                nc.vector.tensor_scalar(ve_a[:, 1], mv_a[:, :, 0], -1.0, None, ALU.mult
                                        ).then_inc(lna_stats, 1)

            def q_low(k):
                for c in range(C):
                    dve.wait_ge(qhi_out, at(k, C, c + 1))
                    if not first(k, 1) and c == 0:
                        dve.wait_ge(q_sent, at(k, 32))
                    nc.vector.tensor_tensor(q_lo[:, c], ps[:, GP + 1 - c], q_hi[:, c], ALU.subtract
                                            ).then_inc(qlo_out, 1)

            def maxima(k, t, lo, hi):
                if t == 0 and lo == 0 and not first(k, 1):
                    dve.wait_ge(mt_done, at(k, 1))
                for p in range(lo, hi):
                    n = t * NP + p
                    dve.wait_ge(max_done, at(k, T * NP, n + 1))
                    nc.vector.tensor_reduce(m_neg[:, t, 2 * p:2 * p + 2],
                                            ps[:, MX + p % 2, 0:2 * SK].rearrange("p (s k) -> p s k", s=2),
                                            X, ALU.max, negate=True).then_inc(max_red, 1)

            def reciprocals(k):
                dve.wait_ge(sums_in, at(k, 16, 16))
                nc.vector.reciprocal(rsum[:, :], sums[:, :]).then_inc(recip, 1)
                dve.wait_ge(recip, at(k, 1, 1))
                if not first(k, 1):
                    dve.wait_ge(rs_sent, at(k, 16))
                nc.vector.tensor_copy(rs_16[:, 0], rsum[:, :]).then_inc(rs_split, 1)
                dve.wait_ge(rs_split, at(k, 2, 1))
                nc.vector.tensor_tensor(rs_16[:, 1], rsum[:, :], rs_16[:, 0], ALU.subtract).then_inc(rs_split, 1)

            def normalise(k):
                dve.wait_ge(a_in[k[1]], at((k[0], 0), 8 * G, 16 * G))
                if not first(k, 1):
                    dve.wait_ge(wo_done, at(k, C))
                for c in range(C):
                    dve.wait_ge(rs_spread, at(k, C, c + 1))
                    nc.vector.tensor_tensor(a_t[:, c], ps[:, GP + c], a_raw[:, c], ALU.mult
                                            ).then_inc(at_ready, 1)

            def add_residual(k, u):
                dve.wait_ge(xbo_ready, at(k, 1, 1))
                dve.wait_ge(wo_done, at(k, C, u + 1))
                if u == 0 and not first(k, 1):
                    dve.wait_ge(x1bf_ready, at(k, 1))
                nc.vector.tensor_tensor(x1[:, 2 * u:2 * u + 2].rearrange("p t c -> p (t c)"), ps[:, GP + u],
                                        x_bo[:, 2 * u:2 * u + 2].rearrange("p t c -> p (t c)"), ALU.add
                                        ).then_inc(x1_ready, 1)

            def ln_c(k):
                dve.wait_ge(x1_ready, at(k, C, C))
                ln_stats(k, x1, st_c, mv_c, lnc_dve)
                nc.vector.tensor_scalar(ve_c[:, :], mv_c[:, :, 1], EPS, None, ALU.add).then_inc(lnc_stats, 1)

            def quantise(k):
                dve.wait_ge(lnc_rstd, at(k, 1, 1))
                if not first(k, 1):
                    dve.wait_ge(xqt_done, at(k, C))
                dve.sem_inc(past_dve, 1)
                for t in range(T):
                    last = nc.vector.tensor_scalar(xq[:, t], x1[:, t], mv_c[:, t, 0:1], rs_c[:, t:t + 1],
                                                   ALU.subtract, ALU.mult, saturate=False)
                last.then_inc(xq_ready, 1)

            nc.vector.memset(q_st[KM - 1:KR], 1.0).then_inc(q_ones, 1)
            nc.vector.memset(v_all[:], 0.0).then_inc(dve_const, 1)
            nc.vector.memset(mask_own[:], 0.0).then_inc(dve_const, 1)
            nc.vector.memset(k_hi[:, :, :, SK:KP], 0.0)
            nc.vector.memset(k_lo[:, :, :, SK:KP], 0.0)
            dve.wait_ge(dve_const, 2)
            v_main = v_all[:, :, 0:H * LW].rearrange("p b (h d e) -> p b h d e", h=H, e=2)
            nc.vector.memset(v_main[:, :, :, :, 1], 1.0 / RS)
            for j in range(4):
                v_left = v_all[32 * j:32 * j + L, :, H * LW:VB].rearrange("p b (g n) -> p b g n", g=G)
                nc.vector.memset(v_left[:, :, :, 32 * j + 1:32 * j + 32:2], 1.0 / RS)

            ln_a((0, 0))
            dve.wait_ge(mask_in_s, 16)
            nc.vector.tensor_copy(keep, mask_in[:]).then_inc(mask_dve, 1)
            dve.wait_ge(mask_dve, 1)
            nc.vector.reduce_max(row_keep[:, :], keep, X).then_inc(mask_dve, 1)
            nc.vector.reduce_max(col_part[:, :], keep.rearrange("p t k -> p k t"), X).then_inc(mask_dve, 1)
            dve.wait_ge(pool_const, 3)
            nc.vector.tensor_copy(ident16[:, :], ident[:, :]).then_inc(dve_const, 1)
            nc.vector.tensor_copy(identb[:, :], ident[:, :]).then_inc(dve_const, 1)
            nc.vector.tensor_scalar(ident8[:, :], ident[:, :], 1.0, None, ALU.mult, saturate=False
                                    ).then_inc(dve_const, 1)
            dve.wait_ge(w_in[4], 16)
            nc.vector.tensor_scalar(wf_small, w_raw[:, 4], 240.0, -240.0, ALU.min, ALU.max)
            nc.vector.tensor_scalar(wf_big, w_raw[:, 4], 448.0, -448.0, ALU.min, ALU.max).then_inc(wf_dve, 1)
            dve.wait_ge(wf_dve, 1)
            nc.vector.tensor_scalar(wf_8[:, 0], wf_small, 1.0, None, ALU.mult, saturate=False)
            nc.vector.tensor_scalar(wf_8[:, 1], wf_big, 0.5, None, ALU.mult, saturate=False
                                    ).then_inc(wf_dve, 1)
            dve.wait_ge(wf_dve, 2)
            nc.vector.tensor_scalar(wf_big, wf_8[:, 1], 2.0, None, ALU.mult).then_inc(wf_dve, 1)
            dve.wait_ge(wf_dve, 3)
            nc.vector.tensor_tensor(wf_big, wf_big, wf_8[:, 0], ALU.subtract)
            nc.vector.tensor_tensor(wf_small, w_raw[:, 4], w_raw[:, 4], ALU.mult).then_inc(wf_dve, 1)
            dve.wait_ge(wf_dve, 4)
            nc.vector.tensor_scalar(wf_small, wf_small, 256.0, None, ALU.is_ge).then_inc(wf_dve, 1)
            dve.wait_ge(wf_dve, 5)
            nc.vector.tensor_tensor(wf_small, wf_small, wf_big, ALU.mult).then_inc(wf_dve, 1)
            dve.wait_ge(wf_dve, 6)
            nc.vector.tensor_tensor(wf_q, wf_8[:, 0], wf_small, ALU.add).then_inc(wf_dve, 1)
            for n in range(2 * C):
                c, s = n // 2, n % 2
                hi, lo = (part[:, c, 2 * s:2 * s + 2, 0:SK] for part in (k_hi, k_lo))
                both = ps[:, n, 0:2 * SK].rearrange("p (b k) -> p b k", b=2)
                dve.wait_ge(pro_pe, 9 + n)
                nc.vector.tensor_copy(hi, both).then_inc(k_split, 1)
                dve.wait_ge(k_split, 2 * n + 1)
                nc.vector.tensor_tensor(lo, both, hi, ALU.subtract).then_inc(k_split, 1)
            dve.wait_ge(mask_pool, 1)
            nc.vector.tensor_scalar(neg_row[:, 0:SK], col_keep[0:1, :], -NEG, NEG, ALU.mult, ALU.add)
            nc.vector.memset(neg_row[:, SK:KP], NEG)
            nc.vector.tensor_tensor(keep, keep, col_keep[:, None, :].to_broadcast([P, ST * T, SK]),
                                    ALU.subtract).then_inc(mask_dve, 1)
            dve.wait_ge(mask_dve, 4)
            nc.vector.tensor_reduce(own_part[:, :], keep, XY, ALU.min, negate=True).then_inc(mask_dve, 1)
            nc.vector.tensor_scalar(mask_own[:, :, 0:SK], keep, -NEG, None, ALU.mult).then_inc(mask_dve, 1)
            for b in range(B):
                dve.wait_ge(pro_pe, 13)
                nc.vector.tensor_copy(v_main[:, b, :, :, 0],
                                      ps[:, 4 + b // 2, (b % 2) * D:(b % 2 + 1) * D].rearrange("p (h d) -> p h d", d=DK))
            dve.wait_ge(pro_pe, 14)
            for b in range(B):
                for j in range(4):
                    v_left = v_all[32 * j:32 * j + L, b, H * LW:VB].rearrange("p (g n) -> p g n", g=G)
                    src = ps[32 * j:32 * j + L, 6 + b // 2, (b % 2) * D:(b % 2 + 1) * D
                             ].rearrange("p (g j d) -> p g j d", g=G, j=4)
                    last = nc.vector.tensor_copy(v_left[:, :, 32 * j:32 * j + 32:2], src[:, :, j])
            last.then_inc(v_built, 1)
            dve.wait_ge(mask_pool, 2)
            nc.vector.tensor_copy(own_flag[:, :], own_any[0:1, :]).then_inc(mask_dve, 1)
            q_low((0, 0))
            ln_a((0, 1))
            for t in range(T):
                maxima((0, 0), t, 0, NP)
            q_low((0, 1))

            def step(k, more=2, back=True):
                j, n, a = ahead(k, -1), ahead(k, 1), ahead(k, 2)
                if more > 0:
                    maxima(n, 0, 0, NP)
                if back:
                    reciprocals(j)
                if more > 1:
                    ln_a(a)
                if more > 0:
                    maxima(n, 1, 0, NP)
                if back:
                    normalise(j)
                if more > 0:
                    maxima(n, 2, 0, NP)
                for u in range(C):
                    if more > 0:
                        maxima(n, 3, 2 * u, 2 * u + 2)
                    if back:
                        add_residual(j, u)
                if back:
                    ln_c(j)
                if more > 0:
                    maxima(n, 3, 4, NP)
                if back:
                    quantise(j)
                if more > 1:
                    q_low(a)

            step((0, 0), back=False)
            step((0, 1))
            with dve.Fori(1, B - 1) as h:
                step((h, 0))
                step((h, 1))
            step((B - 1, 0), more=1)
            step(LAST, more=0)
            reciprocals(LAST)
            normalise(LAST)
            for u in range(C):
                add_residual(LAST, u)
            ln_c(LAST)
            quantise(LAST)

        @block.tensor
        def _(pe):
            pe.wait_ge(pool_const, 7)
            for n, i in enumerate((0, 1, 2, 3)):
                pe.wait_ge(w_in[i], 16)
                for c in range(C):
                    for o in range(C):
                        last = nc.tensor.transpose(ps[:, i, c * D + o * P:c * D + o * P + P],
                                                   w_raw[:, i, o, c * P:c * P + P], ident[:, :])
                last.then_inc(pro_pe, 1)
            pe.wait_ge(ctx_in_s, 16)
            for n in range(4):
                c, s = n // 2, n % 2
                for t in range(4):
                    last = nc.tensor.transpose(ps[:, 4 + n, t * CT:(t + 1) * CT],
                                               ctx_in[:, 4 * s + t, c * P:c * P + P], ident[0:CT, 0:CT])
                last.then_inc(pro_pe, 1)
            pe.wait_ge(pro_act, 8)
            for n in range(2 * C):
                c, s = n // 2, n % 2
                for i in range(C):
                    last = nc.tensor.matmul(ps[:, n, 0:2 * SK], w_t[:, 1, i, c * P:c * P + P],
                                            ctx_t[:, i, s * 2 * SK:(s + 1) * 2 * SK], start=i == 0, stop=i == C - 1)
                last.then_inc(pro_pe, 1)
            for b in range(B):
                for i in range(C):
                    last = nc.tensor.matmul(ps[:, 4 + b // 2, (b % 2) * D:(b % 2 + 1) * D],
                                            ctx_t[:, i, b * SK:b * SK + P], w_t[:, 2, i, :],
                                            start=i == 0, stop=i == C - 1)
            last.then_inc(pro_pe, 1)
            for b in range(B):
                for j in range(4):
                    for i in range(C):
                        last = nc.tensor.matmul(ps[32 * j:32 * j + L, 6 + b // 2, (b % 2) * D:(b % 2 + 1) * D],
                                                ctx_t[:, i, b * SK + P:(b + 1) * SK], w_t[:, 2, i, :],
                                                start=i == 0, stop=i == C - 1)
            last.then_inc(pro_pe, 1)
            pe.wait_ge(wf_dve, 7)
            pe.wait_ge(dve_const, 5)
            pe.wait_ge(k_split, 2)
            for c in range(C):
                for o in range(C):
                    last = nc.tensor.transpose(wf_ps[:, c * D + o * P:c * D + o * P + P],
                                               wf_q[:, o, c * P:c * P + P], identb[:, :])
            last.then_inc(pro_pe, 1)

            def transpose_x(k, previous):
                pe.wait_ge(xn_ready, at(k, 1, 1))
                previous()
                for c in range(C):
                    for t in range(T):
                        last = nc.tensor.transpose(ps[:, GP + 1 - c, t * P:t * P + P],
                                                   xn[:, t, c * P:c * P + P], ident[:, :])
                    last.then_inc(xt_done, 1)

            def project_q(k):
                pe.wait_ge(xt_out, at(k, C, C))
                for c in range(C):
                    if c == 1 and not first(k, 1):
                        pe.wait_ge(mt_out, at(k, 1))
                    for i in range(C):
                        last = nc.tensor.matmul(ps[:, GP + 1 - c], w_t[:, 0, i, c * P:c * P + P], xn_t[:, i],
                                                start=i == 0, stop=i == C - 1)
                    last.then_inc(q_done, 1)

            def transpose_m(k):
                pe.wait_ge(max_red, at(k, T * NP, T * NP))
                for t in range(T):
                    last = nc.tensor.transpose(ps[0:H, GP, t * P:t * P + P], m_neg[:, t], ident[:, :])
                last.then_inc(mt_done, 1)

            def write_out(own):

                def row_scores(k, t, lo, hi):
                    if t == 0 and lo == 0:
                        pe.wait_ge(q_stacked[k[1]], at((k[0], 0), 24, 48))
                        pe.wait_ge(kmax_in, at((k[0], 0), 8, 16))
                    for p in range(lo, hi):
                        n = t * NP + p
                        if not first(k, 1) or n >= 2:
                            pe.wait_ge(max_red, at(k, T * NP, n - 1))
                        dst = ps[:, MX + p % 2, 0:2 * SK]
                        last = nc.tensor.matmul(dst, q_st[0:KM, k[1], p, t * P:t * P + P],
                                                k_max[0:KM, p, :, 0:SK], start=True, stop=not own)
                        if own:
                            last = nc.tensor.matmul(
                                dst, ident16[:, :],
                                mask_own[:, T * k[1] + t, None, 0:SK].to_broadcast([P, 2, SK]),
                                start=False, stop=True)
                        last.then_inc(max_done, 1)

                def scores(k, g, c):
                    n = g * CH + c
                    if n == 0:
                        pe.wait_ge(m_stacked[k[1]], at((k[0], 0), 8, 16))
                        pe.wait_ge(know_in, at((k[0], 0), 8, 16))
                    before = n - 3 if n >= 3 else (18, 19, 17)[n] - G * CH
                    if not first(k, 1) or n >= 3:
                        pe.wait_ge(exp_done, at(k, G * CH, before + 1))
                    bank = ps[:, SC + n % 3]
                    heads = [(c, 0, P, bank)] if c < 4 else [
                        (j, P, KP, ps[32 * j:32 * j + LW, SC + n % 3]) for j in range(4)]
                    for j, lo, hi, dst in heads:
                        last = nc.tensor.matmul(dst, k_now[:, 2 * g + j // 2, j % 2, lo:hi],
                                                q_st[:, k[1], 2 * g + j // 2], start=True, stop=not own)
                        if own:
                            for t in range(T):
                                last = nc.tensor.matmul(dst[:, t * P:t * P + P],
                                                        mask_own[:, T * k[1] + t, lo:hi], ident16[:, :],
                                                        start=False, stop=t == T - 1)
                    last.then_inc(sc_done, 1)

                def values(k, g, c):
                    if c == 0:
                        if not first(k, 1) or g > 0:
                            pe.wait_ge(ot_out, at(k, G, g))
                        if g == 0:
                            pe.wait_ge(vnow_in, at((k[0], 0), 8, 16))
                    pe.wait_ge(exp_done, at(k, G * CH, g * CH + c + 1))
                    if c < 4:
                        h = 4 * g + c
                        nc.tensor.matmul(ps[32 * c:32 * c + LW, OB], v_now[:, h * LW:(h + 1) * LW],
                                         p_t[:, g % 2, c], start=True, stop=False)
                    else:
                        nc.tensor.matmul(ps[:, OB], v_now[:, H * LW + g * P:H * LW + (g + 1) * P],
                                         p_t[:, g % 2, c], start=False, stop=True).then_inc(pv_done, 1)

                def spread_reciprocals(k, q_last):
                    pe.wait_ge(rsrow_in, at(k, 16, 16))
                    if q_last is not None:
                        pe.wait_ge(qlo_out, at(q_last, C, C))
                    if not first(k, 1):
                        pe.wait_ge(ff_out, at(k, C))
                    for c in range(C):
                        nc.tensor.matmul(ps[:, GP + c], spread[:, c], rs_row[:, :], start=True, stop=True
                                         ).then_inc(rs_spread, 1)

                def output(k, u):
                    if u == 0:
                        pe.wait_ge(at_ready, at(k, C, C))
                    for t in (2 * u, 2 * u + 1):
                        for c in range(C):
                            last = nc.tensor.matmul(ps[:, GP + u, (t % 2) * D:(t % 2 + 1) * D],
                                                    a_t[:, c, t * P:t * P + P], w_t[:, 3, c, :],
                                                    start=c == 0, stop=c == C - 1)
                    last.then_inc(wo_done, 1)

                def transpose_xq(k, x_next):
                    pe.wait_ge(xq_ready, at(k, 1, 1))
                    if x_next is not None:
                        pe.wait_ge(xt_out, at(x_next, C, C))
                    pe.sem_inc(past_pe, 1)
                    for c in range(C):
                        for t in range(T):
                            last = nc.tensor.matmul(ps[:, GP + c, t * P:t * P + P], xq[:, t, c * P:c * P + P],
                                                    ident8[:, :], start=True, stop=True)
                        last.then_inc(xqt_done, 1)

                def layer(k, previous):
                    pe.wait_ge(xqt_out, at(k, C, C))
                    previous()
                    for u in range(C):
                        for t in (2 * u, 2 * u + 1):
                            for c in range(C):
                                last = nc.tensor.matmul(ps[:, GP + u, (t % 2) * D:(t % 2 + 1) * D],
                                                        xq_t[:, c, t * P:t * P + P], wf_t[:, c, :],
                                                        start=c == 0, stop=c == C - 1)
                        last.then_inc(ff_done, 1)

                def step(k, more=2, back=True):
                    j, n, a = ahead(k, -1), ahead(k, 1), ahead(k, 2)
                    for c in range(CH):
                        scores(k, 0, c)
                    for g in range(1, G):
                        if back and g == 3:
                            spread_reciprocals(j, n if more > 0 else None)
                        for c in range(CH):
                            scores(k, g, c)
                            if more > 0 and c < 4:
                                row_scores(n, g - 1, c, c + 1)
                        for c in range(CH):
                            values(k, g - 1, c)
                            if more > 0 and c < 4:
                                row_scores(n, g - 1, 4 + c, 5 + c)
                    for u in range(C):
                        if more > 0:
                            row_scores(n, 3, 2 * u, 2 * u + 2)
                        if back:
                            output(j, u)
                    for c in range(CH):
                        values(k, 3, c)
                        if more > 0 and c < 4:
                            row_scores(n, 3, 4 + c, 5 + c)
                    if more > 1:
                        def free():
                            pe.wait_ge(qlo_out, at(n, C, C))
                            if back:
                                pe.wait_ge(x1_ready, at(j, C, C))
                        transpose_x(a, free)
                    if back:
                        transpose_xq(j, a if more > 1 else None)
                    if more > 0:
                        if back:
                            pe.wait_ge(xqt_out, at(j, C, C))
                        elif more > 1:
                            pe.wait_ge(xt_out, at(a, C, C))
                        transpose_m(n)
                    if more > 1:
                        project_q(a)
                    if back:
                        def free():
                            if more > 1:
                                pe.wait_ge(qlo_out, at(a, C, C))
                            elif more > 0:
                                pe.wait_ge(mt_out, at(n, 1, 1))
                        layer(j, free)

                for t in range(T):
                    row_scores((0, 0), t, 0, NP)
                pe.wait_ge(xt_out, 2 * C)
                transpose_m((0, 0))
                project_q((0, 1))
                step((0, 0), back=False)
                step((0, 1))
                with pe.Fori(1, B - 1) as h:
                    step((h, 0))
                    step((h, 1))
                step((B - 1, 0), more=1)
                step(LAST, more=0)
                spread_reciprocals(LAST, None)
                for u in range(C):
                    output(LAST, u)
                transpose_xq(LAST, None)
                layer(LAST, lambda: None)

            pe.wait_ge(v_built, 1)
            pe.wait_ge(pro_act, 9)
            transpose_x((0, 0), lambda: None)
            project_q((0, 0))
            transpose_x((0, 1), lambda: pe.wait_ge(qlo_out, C))
            pe.wait_ge(mask_dve, 7)
            differs = nc.tensor.value_load(own_flag[0:1, 0:1])
            with pe.If(differs > 0):
                write_out(True)
            with pe.Else():
                write_out(False)


_OUT = ((4, 1024, 256), "float32")
_INS = ["x", "ctx_1024", "mask_1x1xSxS2_bk0", "L0_xattn_Wq", "L0_xattn_Wk", "L0_xattn_Wv", "L0_xattn_Wo",
        "L0_xattn_bo", "L0_ffn_weight", "L0_ffn_bias"]


def kernel(**inputs):
    import numpy as _np
    import concourse.bacc as _bacc
    from concourse import mybir as _mybir
    from concourse.bass_utils import run_bass_kernel_spmd as _run

    nc = _bacc.Bacc("TRN2", target_bir_lowering=False, num_devices=1)
    arrays, args = {}, []
    for name in _INS:
        a = _np.ascontiguousarray(inputs[name])
        arrays[f"in_{name}_dram"] = a
        args.append(nc.dram_tensor(f"in_{name}_dram", a.shape, _mybir.dt.from_np(a.dtype), kind="ExternalInput").ap())
    dt = _mybir.dt.from_np(_np.dtype(_OUT[1]))
    args.append(nc.dram_tensor("out_dram", _OUT[0], dt, kind="ExternalOutput").ap())
    xattn_ffn(nc, *args)
    r = _run(nc, [arrays], core_ids=[0])
    return r.results[0]["out_dram"]
```

```python
from contextlib import ExitStack

import concourse.bass as bass
from concourse import mybir

ALU = mybir.AluOpType
ACT = mybir.ActivationFunctionType
X = mybir.AxisListType.X
XY = mybir.AxisListType.XY
F32 = mybir.dt.float32
F16 = mybir.dt.float16
BF16 = mybir.dt.bfloat16
F8 = mybir.dt.float8e4
I32 = mybir.dt.int32
U8 = mybir.dt.uint8
RMAX = bass.bass_isa.ReduceOp.max

P = 128
H = 16
DK = 16
NP = H // 2
G = H // 4
T = 4
R = P * T
LW = 32
KR = 97 + H
KM = 97
NEG = -60000.0
EPS = 1e-5
RS = 64.0
CH = 5


def at(k, per, plus=0):
    return k[0] * (2 * per) + (k[1] * per + plus)


def ahead(k, d):
    n = k[1] + d
    return (k[0] + n // 2, n % 2)


def first(k, d=0):
    return isinstance(k[0], int) and 2 * k[0] + k[1] - d < 0


def xattn_ffn(nc, x, ctx, mask, wq, wk, wv, wo, bo, wf, bf, out):
    B, S, D = x.shape
    SK = ctx.shape[1]
    C = D // P
    L = SK - P
    KP = P + LW
    CT = SK // 2
    NB = B * S // R
    VB = H * LW + G * P
    ST = S // R
    assert D == C * P and D == H * DK and 0 < L <= LW and ST == 2 and CT * 2 == SK and NB == 2 * B

    x_rows = x.rearrange("b (s p t) c -> (b s) p t c", p=P, t=T)
    out_rows = out.rearrange("b (s p t) c -> (b s) p t c", p=P, t=T)
    mask_rows = mask.rearrange("a h (s p t) k -> p s t (a h k)", p=P, t=T)

    q_dram = nc.dram_tensor("q_dram", (2, 2, D, R), F16, kind="Internal").ap()
    k_dram = nc.dram_tensor("k_dram", (2, D, B * KP), F16, kind="Internal").ap()
    s_dram = nc.dram_tensor("s_dram", (H * R,), F32, kind="Internal").ap()
    r_dram = nc.dram_tensor("r_dram", (2, H * R), F16, kind="Internal").ap()

    with ExitStack() as stack:
        def sb(name, shape, dt):
            return stack.enter_context(nc.sbuf_tensor(name, shape, dt))

        def sem(name):
            return stack.enter_context(nc.semaphore(name))

        ident = sb("ident", [P, P], F32)
        ident16 = sb("ident16", [P, P], F16)
        identb = sb("identb", [P, P], BF16)
        ident8 = sb("ident8", [P, P], F8)
        w_t = sb("w_t", [P, 4, C, D], F32)
        wf_t = sb("wf_t", [P, C, D], BF16)
        bo_all = sb("bo_all", [P, D], F32)
        bf_all = sb("bf_all", [P, D], F32)
        half = sb("half", [P, T], F32)
        k_hi = sb("k_hi", [P, C, B, KP], F16)
        k_lo = sb("k_lo", [P, C, B, KP], F16)
        k_all = sb("k_all", [KR, NP, 2, B, KP], F16)
        k_max = sb("k_max", [KR, NP, 2, KP], F16)
        k_now = sb("k_now", [KR, NP, 2, KP], F16)
        v_all = sb("v_all", [P, B, VB], F32)
        v_now = sb("v_now", [P, VB], F32)
        mask_in = sb("mask_in", [P, ST * T, SK], U8)
        row_keep = sb("row_keep", [P, ST * T], F32)
        col_part = sb("col_part", [P, SK], F32)
        col_keep = sb("col_keep", [P, SK], F32)
        mask_own = sb("mask_own", [P, ST * T, KP], F16)
        own_part = sb("own_part", [P, 1], F32)
        own_any = sb("own_any", [P, 1], F32)
        own_flag = sb("own_flag", [1, 1], I32)
        neg_row = sb("neg_row", [1, KP], F16)
        x_a = sb("x_a", [P, 2, T, D], F32)
        st_a = sb("st_a", [P, T, 6], F32)
        mv_a = sb("mv_a", [P, T, 2], F32)
        ve_a = sb("ve_a", [P, 2, T], F32)
        rs_a = sb("rs_a", [P, 3, T], F32)
        xn = sb("xn", [P, T, D], F32)
        xn_t = sb("xn_t", [P, C, R], F32)
        q_hi = sb("q_hi", [P, C, R], F16)
        q_lo = sb("q_lo", [P, C, R], F16)
        q_st = sb("q_st", [KR, 2, NP, R], F16)
        m_neg = sb("m_neg", [P, T, H], F32)
        m_t = sb("m_t", [H, R], F16)
        p_t = sb("p_t", [P, 2, CH, R], F32)
        o_t = sb("o_t", [P, 2, G, R], F32)
        sums = sb("sums", [P, R * H // P], F32)
        rsum = sb("rsum", [P, R * H // P], F32)
        rs_16 = sb("rs_16", [P, 2, R * H // P], F16)
        rs_row = sb("rs_row", [2 * H, R], F16)
        spread = sb("spread", [2 * H, C, P], F16)
        a_raw = sb("a_raw", [P, 2, C, R], F32)
        a_t = sb("a_t", [P, C, R], F32)
        x_c = sb("x_c", [P, 2, T, D], F32)
        x_bo = sb("x_bo", [P, T, D], F32)
        x1 = sb("x1", [P, T, D], F32)
        st_c = sb("st_c", [P, T, 6], F32)
        mv_c = sb("mv_c", [P, T, 2], F32)
        ve_c = sb("ve_c", [P, 2, T], F32)
        rs_c = sb("rs_c", [P, 2, T], F32)
        xq = sb("xq", [P, T, D], F8)
        xq_t = sb("xq_t", [P, C, R], BF16)
        x1_bf = sb("x1_bf", [P, T, D], F32)
        ff = sb("ff", [P, T, D], F16)
        y = sb("y", [P, 2, T, D], F32)

        raw = p_t[:].rearrange("p a c r -> p (a c r)")
        NW = C * D
        w_raw = raw[:, 0:5 * NW].rearrange("p (i o n) -> p i o n", i=5, o=C)
        wf_small = raw[:, 5 * NW:6 * NW].rearrange("p (o n) -> p o n", o=C)
        wf_big = raw[:, 6 * NW:7 * NW].rearrange("p (o n) -> p o n", o=C)
        wf_8 = raw[:, 7 * NW:7 * NW + NW // 2].bitcast(F8).rearrange("p (i o n) -> p i o n", i=2, o=C)
        wf_q = raw[:, 8 * NW:8 * NW + NW // 2].bitcast(BF16).rearrange("p (o n) -> p o n", o=C)
        ctx_in = y[0:CT].rearrange("p a t c -> p (a t) c")
        k_ones = x_c[0:H].rearrange("p a t c -> p (a t c)").bitcast(F16)[:, 0:H * KP].rearrange(
            "p (h k) -> p h k", k=KP)
        spare = o_t[:].rearrange("p a g r -> p (a g r)")
        ctx_t = spare[:, 0:C * B * SK].rearrange("p (c k) -> p c k", c=C)
        keep = spare[:, C * B * SK:C * B * SK + ST * T * SK].rearrange("p (t k) -> p t k", k=SK)

        ps = stack.enter_context(nc.psum_tensor("ps", [P, 8, 512], F32))
        wf_ps = ps[:, 0, 0:C * D // 2].bitcast(BF16)
        SC, OB, MX, GP = 0, 3, 4, 6

        ctx_in_s = sem("ctx_in_s")
        w_in = [sem(f"w_in{i}") for i in range(5)]
        mask_in_s = sem("mask_in_s")
        bias_in = sem("bias_in")
        x_a_in = [sem("x_a_in0"), sem("x_a_in1")]
        x_c_in = [sem("x_c_in0"), sem("x_c_in1")]
        pool_const = sem("pool_const")
        dve_const = sem("dve_const")
        zeroed = sem("zeroed")
        q_ones = sem("q_ones")
        pro_pe = sem("pro_pe")
        pro_act = sem("pro_act")
        k_split = sem("k_split")
        v_built = sem("v_built")
        mask_dve = sem("mask_dve")
        mask_pool = sem("mask_pool")
        wf_dve = sem("wf_dve")
        k_sent = sem("k_sent")
        k_built = sem("k_built")
        kmax_in = sem("kmax_in")
        know_in = sem("know_in")
        vnow_in = sem("vnow_in")
        lna_dve = sem("lna_dve")
        lna_stats = sem("lna_stats")
        lna_pool = sem("lna_pool")
        xn_ready = sem("xn_ready")
        xt_done = sem("xt_done")
        xt_out = sem("xt_out")
        q_done = sem("q_done")
        qhi_out = sem("qhi_out")
        qlo_out = sem("qlo_out")
        q_sent = sem("q_sent")
        q_stacked = [sem("q_stacked0"), sem("q_stacked1")]
        max_done = sem("max_done")
        max_red = sem("max_red")
        mt_done = sem("mt_done")
        mt_out = sem("mt_out")
        m_stacked = [sem("m_stacked0"), sem("m_stacked1")]
        sc_done = sem("sc_done")
        exp_done = sem("exp_done")
        pv_done = sem("pv_done")
        ot_out = sem("ot_out")
        a_in = [sem("a_in0"), sem("a_in1")]
        sums_sent = sem("sums_sent")
        sums_in = sem("sums_in")
        recip = sem("recip")
        rs_split = sem("rs_split")
        rs_sent = sem("rs_sent")
        rsrow_in = sem("rsrow_in")
        rs_spread = sem("rs_spread")
        at_ready = sem("at_ready")
        xbo_ready = sem("xbo_ready")
        wo_done = sem("wo_done")
        x1_ready = sem("x1_ready")
        lnc_dve = sem("lnc_dve")
        lnc_stats = sem("lnc_stats")
        lnc_pool = sem("lnc_pool")
        xq_ready = sem("xq_ready")
        xqt_done = sem("xqt_done")
        xqt_out = sem("xqt_out")
        x1bf_ready = sem("x1bf_ready")
        ff_done = sem("ff_done")
        ff_out = sem("ff_out")
        y_ready = sem("y_ready")
        stored = [sem("stored0"), sem("stored1")]

        past_sp, past_pool, past_act, past_dve, past_pe = (
            sem(f"past_{e}") for e in ("sp", "pool", "act", "dve", "pe"))

        LAST = (B - 1, 1)

        block = stack.enter_context(nc.Block())

        @block.sync
        def _(sp):
            def load_x_a(k):
                if not first(k, 2):
                    sp.wait_ge(xn_ready, at(k, 1, -1))
                sp.sem_inc(past_sp, 1)
                sp.dma_start(x_a[:, k[1]], x_rows[bass.ds(at(k, 1), 1)].rearrange("s p t c -> p (s t) c")
                             ).then_inc(x_a_in[k[1]], 16)

            def send_q(k):
                sp.wait_ge(qhi_out, at(k, C, C))
                sp.wait_ge(qlo_out, at(k, C, C))
                for n, part in enumerate((q_hi, q_lo)):
                    sp.dma_start(q_dram[k[1], n].rearrange("(c p) r -> p c r", p=P), part[:]).then_inc(q_sent, 16)

            def stack_q(k):
                sp.wait_ge(q_sent, at(k, 32, 32))
                if not first(k, 2):
                    sp.sem_inc(past_sp, 1)
                    sp.wait_ge(sc_done, at(k, G * CH, -G * CH))
                for n, part in enumerate((0, 0, 1)):
                    sp.dma_start(q_st[32 * n:32 * n + 32, k[1]],
                                 q_dram[k[1], part].rearrange("(p d) r -> d p r", d=32)
                                 ).then_inc(q_stacked[k[1]], 16)

            def stack_m(k):
                sp.wait_ge(mt_out, at(k, 1, 1))
                sp.dma_start(q_st[KM:KR, k[1]], m_t[:, None, :].to_broadcast([H, NP, R])).then_inc(m_stacked[k[1]], 16)

            def outputs(k, g):
                sp.wait_ge(ot_out, at(k, G, g + 1))
                if g == 0 and not first(k, 2):
                    sp.sem_inc(past_sp, 1)
                    sp.wait_ge(at_ready, at(k, C, -C))
                sp.dma_start(a_raw[64 * (g % 2):64 * (g % 2) + 64, k[1], g // 2], o_t[0:P:2, k[1], g]
                             ).then_inc(a_in[k[1]], 16)

            def gather_sums(k):
                sp.wait_ge(ot_out, at(k, G, G))
                sp.dma_start(s_dram.rearrange("(g i r) -> i g r", i=4, r=R), o_t[1:P:32, k[1]]
                             ).then_inc(sums_sent, 16)
                sp.wait_ge(sums_sent, at(k, 16, 16))
                if not first(k, 1):
                    sp.sem_inc(past_sp, 1)
                    sp.wait_ge(recip, at(k, 1))
                sp.dma_start(sums[:, :], s_dram.rearrange("(p w) -> p w", p=P)).then_inc(sums_in, 16)

            def send_reciprocals(k):
                sp.wait_ge(rs_split, at(k, 2, 2))
                sp.dma_start(r_dram.rearrange("i (p w) -> p i w", p=P), rs_16[:]).then_inc(rs_sent, 16)
                sp.wait_ge(rs_sent, at(k, 16, 16))
                if not first(k, 1):
                    sp.sem_inc(past_sp, 1)
                    sp.wait_ge(rs_spread, at(k, C))
                sp.dma_start(rs_row[:, :], r_dram.rearrange("i (h r) -> (i h) r", r=R)).then_inc(rsrow_in, 16)

            def keys_of(b):
                return k_all[:].rearrange("r p s b k -> r (p s) (b k)")[:, :, bass.ds(b * KP, KP)]

            def k_max_for(b, seen):
                sp.wait_ge(max_done, seen)
                sp.sem_inc(past_sp, 1)
                sp.dma_start(k_max[:].rearrange("r p s k -> r (p s) k"), keys_of(b)).then_inc(kmax_in, 16)

            def k_now_for(b, scored):
                sp.wait_ge(sc_done, scored)
                sp.sem_inc(past_sp, 1)
                sp.dma_start(k_now[:].rearrange("r p s k -> r (p s) k"), keys_of(b)).then_inc(know_in, 16)

            def v_now_for(b, summed):
                sp.wait_ge(pv_done, summed)
                sp.sem_inc(past_sp, 1)
                sp.dma_start(v_now[:, :], v_all[:].rearrange("p b n -> p (b n)")[:, bass.ds(b * VB, VB)]
                             ).then_inc(vnow_in, 16)

            for i, w in ((0, wq), (4, wf)):
                sp.dma_start(w_raw[:, i], w.rearrange("(o p) n -> p o n", p=P)).then_inc(w_in[i], 16)
            load_x_a((0, 0))
            sp.dma_start(mask_in[:, :, :].rearrange("p (s t) k -> p s t k", s=ST), mask_rows
                         ).then_inc(mask_in_s, 16)
            load_x_a((0, 1))
            sp.dma_start(bo_all[:, :], bass.AP(bo.tensor, 0, [[0, P], [1, D]])).then_inc(bias_in, 16)
            sp.dma_start(bf_all[:, :], bass.AP(bf.tensor, 0, [[0, P], [1, D]])).then_inc(bias_in, 16)

            sp.wait_ge(q_ones, 1)
            sp.wait_ge(zeroed, 2)
            sp.wait_ge(k_split, 2 * 2 * C)
            for n, part in enumerate((k_hi, k_lo)):
                sp.dma_start(k_dram[n].rearrange("(c p) k -> p c k", p=P),
                             part[:].rearrange("p c b k -> p c (b k)")).then_inc(k_sent, 16)
            for b in range(B):
                sp.dma_start(k_all[KM:KR, :, :, b].rearrange("r p s k -> r (p s) k"), k_ones).then_inc(k_built, 16)
            sp.wait_ge(k_sent, 32)
            for s in range(2):
                for n, part in enumerate((0, 1, 0)):
                    row = 32 * n + DK * s
                    sp.dma_start(k_all[row:row + DK, :, s].rearrange("r p b k -> r p (b k)"),
                                 k_dram[part].rearrange("(p s d) k -> s d p k", s=2, d=DK)[s]).then_inc(k_built, 16)
            sp.wait_ge(mask_dve, 6)
            src = bass.AP(neg_row[:].tensor, 0, [[KP, 1], [0, B * NP * 2], [1, KP]])
            sp.dma_start(k_all[KM - 1:KM].rearrange("r p s b k -> r (p s b) k"), src).then_inc(k_built, 16)
            sp.wait_ge(k_built, 16 * (B + 2 * 3 + 1))
            sp.dma_start(k_max[:].rearrange("r p s k -> r (p s) k"), keys_of(0)).then_inc(kmax_in, 16)
            send_q((0, 0))
            stack_q((0, 0))
            sp.dma_start(k_now[:].rearrange("r p s k -> r (p s) k"), keys_of(0)).then_inc(know_in, 16)
            sp.wait_ge(v_built, 1)
            sp.dma_start(v_now[:, :], v_all[:, 0]).then_inc(vnow_in, 16)
            send_q((0, 1))
            stack_q((0, 1))
            stack_m((0, 0))

            def step(k, more=2, back=True):
                n, a = ahead(k, 1), ahead(k, 2)
                if more > 1:
                    load_x_a(a)
                if back:
                    send_reciprocals(ahead(k, -1))
                outputs(k, 0)
                outputs(k, 1)
                if more > 1:
                    send_q(a)
                    stack_q(a)
                if more > 0 and k[1] == 1:
                    k_now_for(n[0], at(k, G * CH, G * CH))
                if more > 0:
                    stack_m(n)
                outputs(k, 2)
                if more > 1 and k[1] == 0:
                    k_max_for(a[0], at(n, T * NP, T * NP))
                outputs(k, 3)
                gather_sums(k)
                if more > 0 and k[1] == 1:
                    v_now_for(n[0], at(k, G, G))

            step((0, 0), back=False)
            step((0, 1))
            with sp.Fori(1, B - 1) as h:
                step((h, 0))
                step((h, 1))
            step((B - 1, 0), more=1)
            step(LAST, more=0)
            send_reciprocals(LAST)

        @block.gpsimd
        def _(pool):
            nc.gpsimd.memset(ident[:, :], 0.0).then_inc(pool_const, 1)
            nc.gpsimd.memset(half[:, :], -0.5).then_inc(pool_const, 1)
            pool.wait_ge(pool_const, 2)
            nc.gpsimd.affine_select(out=ident[:, :], in_=ident[:, :], compare_op=ALU.not_equal, fill=1.0,
                                    base=0, pattern=[[-1, P]], channel_multiplier=1).then_inc(pool_const, 1)
            nc.gpsimd.memset(k_all[:].rearrange("r p s b k -> r (p s b k)").bitcast(F32), 0.0
                             ).then_inc(zeroed, 1)
            nc.gpsimd.memset(k_ones, 0.0).then_inc(pool_const, 1)
            pool.wait_ge(pool_const, 4)
            nc.gpsimd.affine_select(out=k_ones, in_=k_ones, compare_op=ALU.not_equal, fill=1.0, base=0,
                                    pattern=[[-1, H], [0, KP]], channel_multiplier=1).then_inc(zeroed, 1)
            nc.gpsimd.memset(spread[:], 0.0).then_inc(pool_const, 1)
            for part in range(2):
                pool.wait_ge(pool_const, 5 + part)
                to = spread[:].rearrange("p c (h d) -> p c h d", d=DK)
                nc.gpsimd.affine_select(out=to, in_=to, compare_op=ALU.not_equal, fill=1.0 / RS, base=-H * part,
                                        pattern=[[-8, C], [-1, 8], [0, DK]], channel_multiplier=1
                                        ).then_inc(pool_const, 1)

            def ln_a(k):
                pool.wait_ge(lna_stats, at(k, 1, 1))
                nc.gpsimd.tensor_tensor(rs_a[:, 0], ve_a[:, 0], half[:, :], ALU.pow).then_inc(lna_pool, 1)
                pool.wait_ge(lna_pool, at(k, 3, 1))
                pool.wait_ge(mask_dve, 2)
                nc.gpsimd.tensor_tensor(rs_a[:, 1], rs_a[:, 0], row_keep[:, T * k[1]:T * k[1] + T], ALU.mult
                                        ).then_inc(lna_pool, 1)
                pool.wait_ge(lna_pool, at(k, 3, 2))
                nc.gpsimd.tensor_tensor(rs_a[:, 2], rs_a[:, 1], ve_a[:, 1], ALU.mult).then_inc(lna_pool, 1)
                pool.wait_ge(lna_pool, at(k, 3, 3))
                if not first(k, 1):
                    pool.wait_ge(xt_done, at(k, C))
                pool.sem_inc(past_pool, 1)
                for t in range(T):
                    last = nc.gpsimd.tensor_scalar(xn[:, t], x_a[:, k[1], t], rs_a[:, 1, t:t + 1],
                                                   rs_a[:, 2, t:t + 1], ALU.mult, ALU.add)
                last.then_inc(xn_ready, 1)

            def load_x_c(k):
                if not first(k, 2):
                    pool.wait_ge(xbo_ready, at(k, 1, -1))
                    pool.sem_inc(past_pool, 1)
                pool.dma_start(x_c[:, k[1]], x_rows[bass.ds(at(k, 1), 1)].rearrange("s p t c -> p (s t) c")
                               ).then_inc(x_c_in[k[1]], 16)

            def residual(k):
                pool.wait_ge(bias_in, 32)
                pool.wait_ge(x_c_in[k[1]], at((k[0], 0), 8, 16))
                if not first(k, 1):
                    pool.wait_ge(x1_ready, at(k, C))
                nc.gpsimd.tensor_tensor(x_bo[:], x_c[:, k[1]], bo_all[:, None, :].to_broadcast([P, T, D]),
                                        ALU.add).then_inc(xbo_ready, 1)

            def ln_c(k):
                pool.wait_ge(lnc_stats, at(k, 1, 1))
                if not first(k, 1):
                    pool.wait_ge(xq_ready, at(k, 1))
                nc.gpsimd.tensor_tensor(rs_c[:, 0], ve_c[:, 0], half[:, :], ALU.pow).then_inc(lnc_pool, 1)
                pool.wait_ge(lnc_pool, at(k, 2, 1))
                nc.gpsimd.tensor_tensor(rs_c[:, 1], rs_c[:, 0], ve_c[:, 1], ALU.mult).then_inc(lnc_pool, 1)
                pool.wait_ge(x1_ready, at(k, C, C))
                if not first(k, 1):
                    pool.wait_ge(y_ready, at(k, 1))
                nc.gpsimd.tensor_tensor(x1_bf[:], x1[:], bf_all[:, None, :].to_broadcast([P, T, D]), ALU.add
                                        ).then_inc(x1bf_ready, 1)

            def finish(k):
                pool.wait_ge(x1bf_ready, at(k, 1, 1))
                pool.wait_ge(ff_out, at(k, C, C))
                if not first(k, 2):
                    pool.wait_ge(stored[k[1]], at((k[0], 0), 8))
                nc.gpsimd.tensor_tensor(y[:, k[1]], x1_bf[:], ff[:], ALU.add).then_inc(y_ready, 1)
                pool.wait_ge(y_ready, at(k, 1, 1))
                pool.sem_inc(past_pool, 1)
                pool.dma_start(out_rows[bass.ds(at(k, 1), 1)].rearrange("s p t c -> p (s t) c"), y[:, k[1]]
                               ).then_inc(stored[k[1]], 16)

            ln_a((0, 0))
            pool.wait_ge(mask_dve, 3)
            nc.gpsimd.partition_all_reduce(col_keep[:, :], col_part[:, :], P, RMAX).then_inc(mask_pool, 1)
            pool.wait_ge(mask_dve, 5)
            nc.gpsimd.partition_all_reduce(own_any[:, :], own_part[:, :], P, RMAX).then_inc(mask_pool, 1)
            ln_a((0, 1))
            pool.wait_ge(k_built, 16 * (B + 2 * 3 + 1))

            def step(k, more=2, back=2):
                load_x_c(k)
                if back > 1:
                    finish(ahead(k, -2))
                if more > 1:
                    ln_a(ahead(k, 2))
                if back > 0:
                    residual(ahead(k, -1))
                    ln_c(ahead(k, -1))

            step((0, 0), back=0)
            step((0, 1), back=1)
            with pool.Fori(1, B - 1) as h:
                step((h, 0))
                step((h, 1))
            step((B - 1, 0), more=1)
            step(LAST, more=0)
            finish(ahead(LAST, -1))
            residual(LAST)
            ln_c(LAST)
            finish(LAST)
            pool.wait_ge(stored[0], 16 * B)
            pool.wait_ge(stored[1], 16 * B)

        @block.scalar
        def _(act):
            act.dma_start(ctx_in, ctx.rearrange("b (u r) c -> r (b u) c", u=2)).then_inc(ctx_in_s, 16)
            for i, w in ((1, wk), (2, wv), (3, wo)):
                act.dma_start(w_raw[:, i], w.rearrange("(o p) n -> p o n", p=P)).then_inc(w_in[i], 16)

            def evacuate(n, dst, src):
                act.wait_ge(pro_pe, n)
                nc.scalar.activation(dst, src, ACT.Copy).then_inc(pro_act, 1)

            for i in range(4):
                evacuate(i + 1, w_t[:, i].rearrange("p c n -> p (c n)"), ps[:, i])
            for n in range(4):
                c, s = n // 2, n % 2
                evacuate(5 + n, ctx_t[:, c, s * 2 * SK:(s + 1) * 2 * SK], ps[:, 4 + n, 0:2 * SK])

            evacuate(15, wf_t[:].rearrange("p c n -> p (c n)"), wf_ps)

            def x_transposed(k):
                for c in range(C):
                    act.wait_ge(xt_done, at(k, C, c + 1))
                    if not first(k, 1) and c == 0:
                        act.wait_ge(q_done, at(k, C))
                    nc.scalar.activation(xn_t[:, c], ps[:, GP + c], ACT.Copy).then_inc(xt_out, 1)

            def q_high(k):
                for c in range(C):
                    act.wait_ge(q_done, at(k, C, c + 1))
                    if not first(k, 1) and c == 0:
                        act.wait_ge(q_sent, at(k, 32))
                    nc.scalar.activation(q_hi[:, c], ps[:, GP + c], ACT.Copy).then_inc(qhi_out, 1)

            def max_transposed(k):
                act.wait_ge(mt_done, at(k, 1, 1))
                if not first(k, 1):
                    j = ahead(k, -1)
                    act.wait_ge(m_stacked[j[1]], at((j[0], 0), 8, 16))
                nc.scalar.activation(m_t[:, :], ps[0:H, MX], ACT.Copy).then_inc(mt_out, 1)

            def exps(k, g):
                if not first(k, 1) or g >= 2:
                    act.wait_ge(pv_done, at(k, G, g - 1))
                for c in range(CH):
                    n = g * CH + c
                    act.wait_ge(sc_done, at(k, G * CH, n + 1))
                    nc.scalar.activation(p_t[:, g % 2, c], ps[:, SC + n % 3], ACT.Exp, scale=DK ** -0.5
                                         ).then_inc(exp_done, 1)

            def heads_out(k, g):
                act.wait_ge(pv_done, at(k, G, g + 1))
                if g == 0 and not first(k, 2):
                    act.wait_ge(a_in[k[1]], at((k[0], 0), 8 * G))
                    act.wait_ge(sums_sent, at(k, 16, -16))
                nc.scalar.activation(o_t[:, k[1], g], ps[:, OB], ACT.Copy).then_inc(ot_out, 1)

            def quantised_transposed(k):
                for c in range(C):
                    act.wait_ge(xqt_done, at(k, C, c + 1))
                    if not first(k, 1) and c == 0:
                        act.wait_ge(ff_done, at(k, C))
                    nc.scalar.activation(xq_t[:, c], ps[:, GP + c], ACT.Copy).then_inc(xqt_out, 1)

            def layer_out(k):
                for u in range(C):
                    act.wait_ge(ff_done, at(k, C, u + 1))
                    if not first(k, 1) and u == 0:
                        act.wait_ge(y_ready, at(k, 1))
                    nc.scalar.activation(ff[:, 2 * u:2 * u + 2].rearrange("p t c -> p (t c)"), ps[:, GP + u],
                                         ACT.Copy).then_inc(ff_out, 1)

            def quantise(k):
                act.wait_ge(lnc_pool, at(k, 2, 2))
                if not first(k, 1):
                    act.wait_ge(xqt_done, at(k, C))
                act.sem_inc(past_act, 1)
                for t in range(T):
                    last = nc.scalar.activation(xq[:, t], x1[:, t], ACT.Identity, bias=rs_c[:, 1, t:t + 1],
                                                scale=rs_c[:, 0, t:t + 1], saturate=False)
                last.then_inc(xq_ready, 1)

            x_transposed((0, 0))
            q_high((0, 0))
            x_transposed((0, 1))
            q_high((0, 1))
            max_transposed((0, 0))

            def step(k, more=2, back=2):
                if back > 1:
                    quantised_transposed(ahead(k, -2))
                    layer_out(ahead(k, -2))
                exps(k, 0)
                exps(k, 1)
                heads_out(k, 0)
                exps(k, 2)
                if more > 1:
                    x_transposed(ahead(k, 2))
                heads_out(k, 1)
                if more > 1:
                    q_high(ahead(k, 2))
                exps(k, 3)
                if more > 0:
                    max_transposed(ahead(k, 1))
                heads_out(k, 2)
                heads_out(k, 3)
                if back > 0:
                    quantise(ahead(k, -1))

            step((0, 0), back=0)
            step((0, 1), back=1)
            with act.Fori(1, B - 1) as h:
                step((h, 0))
                step((h, 1))
            step((B - 1, 0), more=1)
            step(LAST, more=0)
            quantised_transposed(ahead(LAST, -1))
            layer_out(ahead(LAST, -1))
            quantise(LAST)
            quantised_transposed(LAST)
            layer_out(LAST)

        @block.vector
        def _(dve):
            def ln_stats(k, src, stats, mv, done):
                for t in range(T):
                    nc.vector.bn_stats(stats[:, t], src[:, t]).then_inc(done, 1)
                for t in range(T):
                    dve.wait_ge(done, at(k, 2 * T, t + 1))
                    dve.sem_inc(past_dve, 1)
                    nc.vector.bn_aggr(mv[:, t], stats[:, t]).then_inc(done, 1)
                dve.wait_ge(done, at(k, 2 * T, 2 * T))

            def ln_a(k):
                dve.wait_ge(x_a_in[k[1]], at((k[0], 0), 8, 16))
                ln_stats(k, x_a[:, k[1]], st_a, mv_a, lna_dve)
                if not first(k, 1):
                    dve.wait_ge(lna_pool, at(k, 3))
                nc.vector.tensor_scalar(ve_a[:, 0], mv_a[:, :, 1], EPS, None, ALU.add)
                nc.vector.tensor_scalar(ve_a[:, 1], mv_a[:, :, 0], -1.0, None, ALU.mult
                                        ).then_inc(lna_stats, 1)

            def q_low(k, c):
                dve.wait_ge(qhi_out, at(k, C, c + 1))
                if not first(k, 1) and c == 0:
                    dve.wait_ge(q_sent, at(k, 32))
                nc.vector.tensor_tensor(q_lo[:, c], ps[:, GP + c], q_hi[:, c], ALU.subtract
                                        ).then_inc(qlo_out, 1)

            def maxima(k, t, lo, hi):
                if t == 0 and lo == 0 and not first(k, 1):
                    dve.wait_ge(mt_done, at(k, 1))
                for p in range(lo, hi):
                    n = t * NP + p
                    dve.wait_ge(max_done, at(k, T * NP, n + 1))
                    nc.vector.tensor_reduce(m_neg[:, t, 2 * p:2 * p + 2],
                                            ps[:, MX + p % 2, 0:2 * SK].rearrange("p (s k) -> p s k", s=2),
                                            X, ALU.max, negate=True).then_inc(max_red, 1)

            def reciprocals(k):
                dve.wait_ge(sums_in, at(k, 16, 16))
                nc.vector.reciprocal(rsum[:, :], sums[:, :]).then_inc(recip, 1)
                dve.wait_ge(recip, at(k, 1, 1))
                if not first(k, 1):
                    dve.wait_ge(rs_sent, at(k, 16))
                nc.vector.tensor_copy(rs_16[:, 0], rsum[:, :]).then_inc(rs_split, 1)
                dve.wait_ge(rs_split, at(k, 2, 1))
                nc.vector.tensor_tensor(rs_16[:, 1], rsum[:, :], rs_16[:, 0], ALU.subtract).then_inc(rs_split, 1)

            def normalise(k):
                dve.wait_ge(a_in[k[1]], at((k[0], 0), 8 * G, 16 * G))
                if not first(k, 1):
                    dve.wait_ge(wo_done, at(k, C))
                for c in range(C):
                    dve.wait_ge(rs_spread, at(k, C, c + 1))
                    nc.vector.tensor_tensor(a_t[:, c], ps[:, GP + c], a_raw[:, k[1], c], ALU.mult
                                            ).then_inc(at_ready, 1)

            def add_residual(k, u):
                dve.wait_ge(xbo_ready, at(k, 1, 1))
                dve.wait_ge(wo_done, at(k, C, u + 1))
                if u == 0 and not first(k, 1):
                    dve.wait_ge(x1bf_ready, at(k, 1))
                nc.vector.tensor_tensor(x1[:, 2 * u:2 * u + 2].rearrange("p t c -> p (t c)"), ps[:, GP + u],
                                        x_bo[:, 2 * u:2 * u + 2].rearrange("p t c -> p (t c)"), ALU.add
                                        ).then_inc(x1_ready, 1)

            def ln_c(k):
                dve.wait_ge(x1_ready, at(k, C, C))
                ln_stats(k, x1, st_c, mv_c, lnc_dve)
                if not first(k, 1):
                    dve.wait_ge(lnc_pool, at(k, 2))
                nc.vector.tensor_scalar(ve_c[:, 0], mv_c[:, :, 1], EPS, None, ALU.add)
                nc.vector.tensor_scalar(ve_c[:, 1], mv_c[:, :, 0], -1.0, None, ALU.mult
                                        ).then_inc(lnc_stats, 1)

            nc.vector.memset(q_st[KM - 1:KR], 1.0).then_inc(q_ones, 1)
            nc.vector.memset(v_all[:], 0.0).then_inc(dve_const, 1)
            nc.vector.memset(mask_own[:], 0.0).then_inc(dve_const, 1)
            nc.vector.memset(k_hi[:, :, :, SK:KP], 0.0)
            nc.vector.memset(k_lo[:, :, :, SK:KP], 0.0)
            dve.wait_ge(dve_const, 2)
            v_main = v_all[:, :, 0:H * LW].rearrange("p b (h d e) -> p b h d e", h=H, e=2)
            nc.vector.memset(v_main[:, :, :, :, 1], 1.0 / RS)
            for j in range(4):
                v_left = v_all[32 * j:32 * j + L, :, H * LW:VB].rearrange("p b (g n) -> p b g n", g=G)
                nc.vector.memset(v_left[:, :, :, 32 * j + 1:32 * j + 32:2], 1.0 / RS)

            ln_a((0, 0))
            dve.wait_ge(mask_in_s, 16)
            nc.vector.tensor_copy(keep, mask_in[:]).then_inc(mask_dve, 1)
            dve.wait_ge(mask_dve, 1)
            nc.vector.reduce_max(row_keep[:, :], keep, X).then_inc(mask_dve, 1)
            nc.vector.reduce_max(col_part[:, :], keep.rearrange("p t k -> p k t"), X).then_inc(mask_dve, 1)
            dve.wait_ge(pool_const, 3)
            nc.vector.tensor_copy(ident16[:, :], ident[:, :]).then_inc(dve_const, 1)
            nc.vector.tensor_copy(identb[:, :], ident[:, :]).then_inc(dve_const, 1)
            nc.vector.tensor_scalar(ident8[:, :], ident[:, :], 1.0, None, ALU.mult, saturate=False
                                    ).then_inc(dve_const, 1)
            dve.wait_ge(w_in[4], 16)
            nc.vector.tensor_scalar(wf_small, w_raw[:, 4], 240.0, -240.0, ALU.min, ALU.max)
            nc.vector.tensor_scalar(wf_big, w_raw[:, 4], 448.0, -448.0, ALU.min, ALU.max).then_inc(wf_dve, 1)
            dve.wait_ge(wf_dve, 1)
            nc.vector.tensor_scalar(wf_8[:, 0], wf_small, 1.0, None, ALU.mult, saturate=False)
            nc.vector.tensor_scalar(wf_8[:, 1], wf_big, 0.5, None, ALU.mult, saturate=False
                                    ).then_inc(wf_dve, 1)
            dve.wait_ge(wf_dve, 2)
            nc.vector.tensor_scalar(wf_big, wf_8[:, 1], 2.0, None, ALU.mult).then_inc(wf_dve, 1)
            dve.wait_ge(wf_dve, 3)
            nc.vector.tensor_tensor(wf_big, wf_big, wf_8[:, 0], ALU.subtract)
            nc.vector.tensor_tensor(wf_small, w_raw[:, 4], w_raw[:, 4], ALU.mult).then_inc(wf_dve, 1)
            dve.wait_ge(wf_dve, 4)
            nc.vector.tensor_scalar(wf_small, wf_small, 256.0, None, ALU.is_ge).then_inc(wf_dve, 1)
            dve.wait_ge(wf_dve, 5)
            nc.vector.tensor_tensor(wf_small, wf_small, wf_big, ALU.mult).then_inc(wf_dve, 1)
            dve.wait_ge(wf_dve, 6)
            nc.vector.tensor_tensor(wf_q, wf_8[:, 0], wf_small, ALU.add).then_inc(wf_dve, 1)
            for n in range(2 * C):
                c, s = n // 2, n % 2
                hi, lo = (part[:, c, 2 * s:2 * s + 2, 0:SK] for part in (k_hi, k_lo))
                both = ps[:, n, 0:2 * SK].rearrange("p (b k) -> p b k", b=2)
                dve.wait_ge(pro_pe, 9 + n)
                nc.vector.tensor_copy(hi, both).then_inc(k_split, 1)
                dve.wait_ge(k_split, 2 * n + 1)
                nc.vector.tensor_tensor(lo, both, hi, ALU.subtract).then_inc(k_split, 1)
            dve.wait_ge(mask_pool, 1)
            nc.vector.tensor_scalar(neg_row[:, 0:SK], col_keep[0:1, :], -NEG, NEG, ALU.mult, ALU.add)
            nc.vector.memset(neg_row[:, SK:KP], NEG)
            nc.vector.tensor_tensor(keep, keep, col_keep[:, None, :].to_broadcast([P, ST * T, SK]),
                                    ALU.subtract).then_inc(mask_dve, 1)
            dve.wait_ge(mask_dve, 4)
            nc.vector.tensor_reduce(own_part[:, :], keep, XY, ALU.min, negate=True).then_inc(mask_dve, 1)
            nc.vector.tensor_scalar(mask_own[:, :, 0:SK], keep, -NEG, None, ALU.mult).then_inc(mask_dve, 1)
            for b in range(B):
                dve.wait_ge(pro_pe, 13)
                nc.vector.tensor_copy(v_main[:, b, :, :, 0],
                                      ps[:, 4 + b // 2, (b % 2) * D:(b % 2 + 1) * D].rearrange("p (h d) -> p h d", d=DK))
            dve.wait_ge(pro_pe, 14)
            for b in range(B):
                for j in range(4):
                    v_left = v_all[32 * j:32 * j + L, b, H * LW:VB].rearrange("p (g n) -> p g n", g=G)
                    src = ps[32 * j:32 * j + L, 6 + b // 2, (b % 2) * D:(b % 2 + 1) * D
                             ].rearrange("p (g j d) -> p g j d", g=G, j=4)
                    last = nc.vector.tensor_copy(v_left[:, :, 32 * j:32 * j + 32:2], src[:, :, j])
            last.then_inc(v_built, 1)
            dve.wait_ge(mask_pool, 2)
            nc.vector.tensor_copy(own_flag[:, :], own_any[0:1, :]).then_inc(mask_dve, 1)
            ln_a((0, 1))
            for c in range(C):
                q_low((0, 0), c)
            for c in range(C):
                q_low((0, 1), c)
            for t in range(T):
                maxima((0, 0), t, 0, NP)

            def step(k, more=2, back=True):
                j, n, a = ahead(k, -1), ahead(k, 1), ahead(k, 2)
                if more > 0:
                    maxima(n, 0, 0, NP)
                    maxima(n, 1, 0, 4)
                if back:
                    reciprocals(j)
                if more > 1:
                    ln_a(a)
                if more > 0:
                    maxima(n, 1, 4, NP)
                    maxima(n, 2, 0, NP)
                for c in range(C):
                    if more > 0:
                        maxima(n, 3, 2 * c, 2 * c + 2)
                    if more > 1:
                        q_low(a, c)
                if more > 0:
                    maxima(n, 3, 4, NP)
                if back:
                    normalise(j)
                    for u in range(C):
                        add_residual(j, u)
                    ln_c(j)

            step((0, 0), back=False)
            step((0, 1))
            with dve.Fori(1, B - 1) as h:
                step((h, 0))
                step((h, 1))
            step((B - 1, 0), more=1)
            step(LAST, more=0)
            reciprocals(LAST)
            normalise(LAST)
            for u in range(C):
                add_residual(LAST, u)
            ln_c(LAST)

        @block.tensor
        def _(pe):
            pe.wait_ge(pool_const, 7)
            for n, i in enumerate((0, 1, 2, 3)):
                pe.wait_ge(w_in[i], 16)
                for c in range(C):
                    for o in range(C):
                        last = nc.tensor.transpose(ps[:, i, c * D + o * P:c * D + o * P + P],
                                                   w_raw[:, i, o, c * P:c * P + P], ident[:, :])
                last.then_inc(pro_pe, 1)
            pe.wait_ge(ctx_in_s, 16)
            for n in range(4):
                c, s = n // 2, n % 2
                for t in range(4):
                    last = nc.tensor.transpose(ps[:, 4 + n, t * CT:(t + 1) * CT],
                                               ctx_in[:, 4 * s + t, c * P:c * P + P], ident[0:CT, 0:CT])
                last.then_inc(pro_pe, 1)
            pe.wait_ge(pro_act, 8)
            for n in range(2 * C):
                c, s = n // 2, n % 2
                for i in range(C):
                    last = nc.tensor.matmul(ps[:, n, 0:2 * SK], w_t[:, 1, i, c * P:c * P + P],
                                            ctx_t[:, i, s * 2 * SK:(s + 1) * 2 * SK], start=i == 0, stop=i == C - 1)
                last.then_inc(pro_pe, 1)
            for b in range(B):
                for i in range(C):
                    last = nc.tensor.matmul(ps[:, 4 + b // 2, (b % 2) * D:(b % 2 + 1) * D],
                                            ctx_t[:, i, b * SK:b * SK + P], w_t[:, 2, i, :],
                                            start=i == 0, stop=i == C - 1)
            last.then_inc(pro_pe, 1)
            for b in range(B):
                for j in range(4):
                    for i in range(C):
                        last = nc.tensor.matmul(ps[32 * j:32 * j + L, 6 + b // 2, (b % 2) * D:(b % 2 + 1) * D],
                                                ctx_t[:, i, b * SK + P:(b + 1) * SK], w_t[:, 2, i, :],
                                                start=i == 0, stop=i == C - 1)
            last.then_inc(pro_pe, 1)
            pe.wait_ge(wf_dve, 7)
            pe.wait_ge(dve_const, 5)
            pe.wait_ge(k_split, 2)
            for c in range(C):
                for o in range(C):
                    last = nc.tensor.transpose(wf_ps[:, c * D + o * P:c * D + o * P + P],
                                               wf_q[:, o, c * P:c * P + P], identb[:, :])
            last.then_inc(pro_pe, 1)

            def transpose_x(k):
                pe.wait_ge(xn_ready, at(k, 1, 1))
                if not first(k, 4):
                    pe.wait_ge(ff_out, at(k, C, -3 * C))
                elif not first(k, 1):
                    pe.wait_ge(qlo_out, at(k, C))
                for c in range(C):
                    for t in range(T):
                        last = nc.tensor.transpose(ps[:, GP + c, t * P:t * P + P],
                                                   xn[:, t, c * P:c * P + P], ident[:, :])
                    last.then_inc(xt_done, 1)

            def project_q(k, c):
                if c == 0:
                    pe.wait_ge(xt_out, at(k, C, C))
                for i in range(C):
                    last = nc.tensor.matmul(ps[:, GP + c], w_t[:, 0, i, c * P:c * P + P], xn_t[:, i],
                                            start=i == 0, stop=i == C - 1)
                last.then_inc(q_done, 1)

            def transpose_m(k):
                pe.wait_ge(max_red, at(k, T * NP, T * NP))
                for t in range(T):
                    last = nc.tensor.transpose(ps[0:H, MX, t * P:t * P + P], m_neg[:, t], ident[:, :])
                last.then_inc(mt_done, 1)

            def write_out(own):

                def row_scores(k, t, lo, hi):
                    if t == 0 and lo == 0:
                        if not first(k, 1):
                            pe.wait_ge(mt_out, at(k, 1))
                        pe.wait_ge(q_stacked[k[1]], at((k[0], 0), 24, 48))
                        pe.wait_ge(kmax_in, at((k[0], 0), 8, 16))
                    for p in range(lo, hi):
                        n = t * NP + p
                        if not first(k, 1) or n >= 2:
                            pe.wait_ge(max_red, at(k, T * NP, n - 1))
                        dst = ps[:, MX + p % 2, 0:2 * SK]
                        last = nc.tensor.matmul(dst, q_st[0:KM, k[1], p, t * P:t * P + P],
                                                k_max[0:KM, p, :, 0:SK], start=True, stop=not own)
                        if own:
                            last = nc.tensor.matmul(
                                dst, ident16[:, :],
                                mask_own[:, T * k[1] + t, None, 0:SK].to_broadcast([P, 2, SK]),
                                start=False, stop=True)
                        last.then_inc(max_done, 1)

                def scores(k, g, c):
                    n = g * CH + c
                    if n == 0:
                        pe.wait_ge(m_stacked[k[1]], at((k[0], 0), 8, 16))
                        pe.wait_ge(know_in, at((k[0], 0), 8, 16))
                    before = n - 3 if n >= 3 else (18, 19, 17)[n] - G * CH
                    if not first(k, 1) or n >= 3:
                        pe.wait_ge(exp_done, at(k, G * CH, before + 1))
                    bank = ps[:, SC + n % 3]
                    heads = [(c, 0, P, bank)] if c < 4 else [
                        (j, P, KP, ps[32 * j:32 * j + LW, SC + n % 3]) for j in range(4)]
                    for j, lo, hi, dst in heads:
                        last = nc.tensor.matmul(dst, k_now[:, 2 * g + j // 2, j % 2, lo:hi],
                                                q_st[:, k[1], 2 * g + j // 2], start=True, stop=not own)
                        if own:
                            for t in range(T):
                                last = nc.tensor.matmul(dst[:, t * P:t * P + P],
                                                        mask_own[:, T * k[1] + t, lo:hi], ident16[:, :],
                                                        start=False, stop=t == T - 1)
                    last.then_inc(sc_done, 1)

                def values(k, g, c):
                    if c == 0:
                        if not first(k, 1) or g > 0:
                            pe.wait_ge(ot_out, at(k, G, g))
                        if g == 0:
                            pe.wait_ge(vnow_in, at((k[0], 0), 8, 16))
                    pe.wait_ge(exp_done, at(k, G * CH, g * CH + c + 1))
                    if c < 4:
                        h = 4 * g + c
                        nc.tensor.matmul(ps[32 * c:32 * c + LW, OB], v_now[:, h * LW:(h + 1) * LW],
                                         p_t[:, g % 2, c], start=True, stop=False)
                    else:
                        nc.tensor.matmul(ps[:, OB], v_now[:, H * LW + g * P:H * LW + (g + 1) * P],
                                         p_t[:, g % 2, c], start=False, stop=True).then_inc(pv_done, 1)

                def spread_reciprocals(k, q_last):
                    pe.wait_ge(rsrow_in, at(k, 16, 16))
                    if q_last is not None:
                        pe.wait_ge(qlo_out, at(q_last, C, C))
                    elif not first(k, 1):
                        pe.wait_ge(ff_out, at(k, C))
                    for c in range(C):
                        nc.tensor.matmul(ps[:, GP + c], spread[:, c], rs_row[:, :], start=True, stop=True
                                         ).then_inc(rs_spread, 1)

                def output(k, u):
                    if u == 0:
                        pe.wait_ge(at_ready, at(k, C, C))
                    for t in (2 * u, 2 * u + 1):
                        for c in range(C):
                            last = nc.tensor.matmul(ps[:, GP + u, (t % 2) * D:(t % 2 + 1) * D],
                                                    a_t[:, c, t * P:t * P + P], w_t[:, 3, c, :],
                                                    start=c == 0, stop=c == C - 1)
                    last.then_inc(wo_done, 1)

                def transpose_xq(k):
                    pe.wait_ge(xq_ready, at(k, 1, 1))
                    pe.sem_inc(past_pe, 1)
                    for c in range(C):
                        for t in range(T):
                            last = nc.tensor.matmul(ps[:, GP + c, t * P:t * P + P], xq[:, t, c * P:c * P + P],
                                                    ident8[:, :], start=True, stop=True)
                        last.then_inc(xqt_done, 1)

                def layer(k):
                    pe.wait_ge(xqt_out, at(k, C, C))
                    for u in range(C):
                        for t in (2 * u, 2 * u + 1):
                            for c in range(C):
                                last = nc.tensor.matmul(ps[:, GP + u, (t % 2) * D:(t % 2 + 1) * D],
                                                        xq_t[:, c, t * P:t * P + P], wf_t[:, c, :],
                                                        start=c == 0, stop=c == C - 1)
                        last.then_inc(ff_done, 1)

                def step(k, more=2, back=2):
                    i, j, n, a = ahead(k, -2), ahead(k, -1), ahead(k, 1), ahead(k, 2)

                    def search(t, lo, hi):
                        if more > 0:
                            row_scores(n, t, lo, hi)

                    if back > 1:
                        transpose_xq(i)
                    search(0, 0, 4)
                    if back > 1:
                        layer(i)
                    for c in range(CH):
                        scores(k, 0, c)
                        if c < 4:
                            search(0, 4 + c, 5 + c)
                    for c in range(CH):
                        scores(k, 1, c)
                        if c < 4:
                            search(1, c, c + 1)
                    for c in range(CH):
                        values(k, 0, c)
                        if c < 4:
                            search(1, 4 + c, 5 + c)
                    for c in range(CH):
                        scores(k, 2, c)
                        if c < 4:
                            search(2, c, c + 1)
                    if more > 1:
                        transpose_x(a)
                    for c in range(CH):
                        values(k, 1, c)
                        if c < 4:
                            search(2, 4 + c, 5 + c)
                    for c in range(C):
                        if more > 1:
                            project_q(a, c)
                        search(3, 2 * c, 2 * c + 2)
                    for c in range(CH):
                        scores(k, 3, c)
                        if c < 4:
                            search(3, 4 + c, 5 + c)
                    if back > 0:
                        spread_reciprocals(j, a if more > 1 else None)
                        for u in range(C):
                            output(j, u)
                    if more > 0:
                        transpose_m(n)
                    for g in (2, 3):
                        for c in range(CH):
                            values(k, g, c)

                for t in range(T):
                    row_scores((0, 0), t, 0, NP)
                transpose_m((0, 0))
                step((0, 0), back=0)
                step((0, 1), back=1)
                with pe.Fori(1, B - 1) as h:
                    step((h, 0))
                    step((h, 1))
                step((B - 1, 0), more=1)
                step(LAST, more=0)
                transpose_xq(ahead(LAST, -1))
                layer(ahead(LAST, -1))
                spread_reciprocals(LAST, None)
                for u in range(C):
                    output(LAST, u)
                transpose_xq(LAST)
                layer(LAST)

            pe.wait_ge(v_built, 1)
            pe.wait_ge(pro_act, 9)
            for k in ((0, 0), (0, 1)):
                transpose_x(k)
                for c in range(C):
                    project_q(k, c)
            pe.wait_ge(mask_dve, 7)
            differs = nc.tensor.value_load(own_flag[0:1, 0:1])
            with pe.If(differs > 0):
                write_out(True)
            with pe.Else():
                write_out(False)


_OUT = ((4, 1024, 256), "float32")
_INS = ["x", "ctx_1024", "mask_1x1xSxS2_bk0", "L0_xattn_Wq", "L0_xattn_Wk", "L0_xattn_Wv", "L0_xattn_Wo",
        "L0_xattn_bo", "L0_ffn_weight", "L0_ffn_bias"]


def kernel(**inputs):
    import numpy as _np
    import concourse.bacc as _bacc
    from concourse import mybir as _mybir
    from concourse.bass_utils import run_bass_kernel_spmd as _run

    nc = _bacc.Bacc("TRN2", target_bir_lowering=False, num_devices=1)
    arrays, args = {}, []
    for name in _INS:
        a = _np.ascontiguousarray(inputs[name])
        arrays[f"in_{name}_dram"] = a
        args.append(nc.dram_tensor(f"in_{name}_dram", a.shape, _mybir.dt.from_np(a.dtype), kind="ExternalInput").ap())
    dt = _mybir.dt.from_np(_np.dtype(_OUT[1]))
    args.append(nc.dram_tensor("out_dram", _OUT[0], dt, kind="ExternalOutput").ap())
    xattn_ffn(nc, *args)
    r = _run(nc, [arrays], core_ids=[0])
    return r.results[0]["out_dram"]
```

```python
from contextlib import ExitStack

import concourse.bass as bass
from concourse import mybir

ALU = mybir.AluOpType
ACT = mybir.ActivationFunctionType
X = mybir.AxisListType.X
XY = mybir.AxisListType.XY
F32 = mybir.dt.float32
F16 = mybir.dt.float16
BF16 = mybir.dt.bfloat16
F8 = mybir.dt.float8e4
I32 = mybir.dt.int32
U8 = mybir.dt.uint8
RMAX = bass.bass_isa.ReduceOp.max

P = 128
H = 16
DK = 16
NP = H // 2
G = H // 4
T = 4
R = P * T
LW = 32
KR = 97 + H
KM = 97
NEG = -60000.0
EPS = 1e-5
RS = 64.0
SB = 2
MB = 3
WARM_IN = 14
WARM_OUT = 24
ZX = 10
ZX_0 = 10
ZC = 14
LAG = 3
NU = T * NP
EARLY = 26
WITH = (1, 3, 2, 2, 2, 1, 1, 4, 2, 2, 3, 1, 5, 2, 1, 0, 0, 0, 0, 0)
WITH_0 = (0, 0, 2, 2, 2, 2, 2, 3, 2, 2, 3, 2, 5, 3, 2, 0, 0, 0, 0, 0)
MZ = 15
CH = 5
NC = G * CH


def units(with_z, z, part=0, parts=1):
    lo, n = sum(with_z[:z]), with_z[z]
    return range(lo + n * part // parts, lo + n * (part + 1) // parts)


def at(k, per, plus=0):
    return k[0] * (2 * per) + (k[1] * per + plus)


def ahead(k, d):
    n = k[1] + d
    return (k[0] + n // 2, n % 2)


def first(k, d=0):
    return isinstance(k[0], int) and 2 * k[0] + k[1] - d < 0


def xattn_ffn(nc, x, ctx, mask, wq, wk, wv, wo, bo, wf, bf, out):
    B, S, D = x.shape
    SK = ctx.shape[1]
    C = D // P
    L = SK - P
    KP = P + LW
    CT = SK // 2
    NB = B * S // R
    VB = H * LW + G * P
    ST = S // R
    assert D == C * P and D == H * DK and 0 < L <= LW and ST == 2 and CT * 2 == SK and NB == 2 * B

    x_rows = x.rearrange("b (s p t) c -> (b s) p t c", p=P, t=T)
    out_rows = out.rearrange("b (s p t) c -> (b s) p t c", p=P, t=T)
    mask_rows = mask.rearrange("a h (s p t) k -> p s t (a h k)", p=P, t=T)

    q_dram = nc.dram_tensor("q_dram", (2, 2, D, R), F16, kind="Internal").ap()
    k_dram = nc.dram_tensor("k_dram", (2, D, B * KP), F16, kind="Internal").ap()
    s_dram = nc.dram_tensor("s_dram", (H * R,), F32, kind="Internal").ap()
    r_dram = nc.dram_tensor("r_dram", (2, H * R), F16, kind="Internal").ap()

    with ExitStack() as stack:
        def sb(name, shape, dt):
            return stack.enter_context(nc.sbuf_tensor(name, shape, dt))

        def sem(name):
            return stack.enter_context(nc.semaphore(name))

        ident = sb("ident", [P, P], F32)
        ident16 = sb("ident16", [P, P], F16)
        identb = sb("identb", [P, P], BF16)
        ident8 = sb("ident8", [P, P], F8)
        w_t = sb("w_t", [P, 4, C, D], F32)
        wf_t = sb("wf_t", [P, C, D], BF16)
        bo_all = sb("bo_all", [P, D], F32)
        bf_all = sb("bf_all", [P, D], F32)
        half = sb("half", [P, T], F32)
        k_hi = sb("k_hi", [P, C, B, KP], F16)
        k_lo = sb("k_lo", [P, C, B, KP], F16)
        k_all = sb("k_all", [KR, NP, 2, B, KP], F16)
        k_max = sb("k_max", [KR, NP, 2, KP], F16)
        k_now = sb("k_now", [KR, NP, 2, KP], F16)
        v_all = sb("v_all", [P, B, VB], F32)
        v_now = sb("v_now", [P, VB], F32)
        mask_in = sb("mask_in", [P, ST * T, SK], U8)
        row_keep = sb("row_keep", [P, ST * T], F32)
        col_part = sb("col_part", [P, SK], F32)
        col_keep = sb("col_keep", [P, SK], F32)
        mask_own = sb("mask_own", [P, ST * T, KP], F16)
        own_part = sb("own_part", [P, 1], F32)
        own_any = sb("own_any", [P, 1], F32)
        own_flag = sb("own_flag", [1, 1], I32)
        one_row = sb("one_row", [H, R], F16)
        neg_row = sb("neg_row", [1, KP], F16)
        x_a = sb("x_a", [P, 2, T, D], F32)
        st_a = sb("st_a", [P, T, 6], F32)
        mv_a = sb("mv_a", [P, T, 2], F32)
        ve_a = sb("ve_a", [P, 2, T], F32)
        rs_a = sb("rs_a", [P, 3, T], F32)
        xn = sb("xn", [P, T, D], F32)
        xn_t = sb("xn_t", [P, C, R], F32)
        q_hi = sb("q_hi", [P, C, R], F16)
        q_lo = sb("q_lo", [P, C, R], F16)
        q_st = sb("q_st", [KR, 2, NP, R], F16)
        m_neg = sb("m_neg", [P, T, H], F32)
        m_t = sb("m_t", [H, R], F16)
        p_t = sb("p_t", [P, 2, CH, R], F32)
        o_t = sb("o_t", [P, 2, G, R], F32)
        sums = sb("sums", [P, R * H // P], F32)
        rsum = sb("rsum", [P, R * H // P], F32)
        rs_16 = sb("rs_16", [P, 2, R * H // P], F16)
        rs_row = sb("rs_row", [2 * H, R], F16)
        spread = sb("spread", [2 * H, C, P], F16)
        a_raw = sb("a_raw", [P, 2, C, R], F32)
        a_t = sb("a_t", [P, C, R], F32)
        x_c = sb("x_c", [P, 2, T, D], F32)
        x_bo = sb("x_bo", [P, T, D], F32)
        x1 = sb("x1", [P, T, D], F32)
        st_c = sb("st_c", [P, T, 6], F32)
        mv_c = sb("mv_c", [P, T, 2], F32)
        ve_c = sb("ve_c", [P, 2, T], F32)
        rs_c = sb("rs_c", [P, 2, T], F32)
        xq = sb("xq", [P, T, D], F8)
        xq_t = sb("xq_t", [P, C, R], BF16)
        x1_bf = sb("x1_bf", [P, T, D], F32)
        ff = sb("ff", [P, T, D], F16)
        y = sb("y", [P, 2, T, D], F32)

        raw = p_t[:].rearrange("p a c r -> p (a c r)")
        NW = C * D
        w_raw = raw[:, 0:4 * NW].rearrange("p (i o n) -> p i o n", i=4, o=C)
        x1_flat, bf_flat = (a[:].rearrange("p t c -> p (t c)") for a in (x1, x1_bf))
        wf_raw, wf_small = (x1_flat[:, i * NW:(i + 1) * NW].rearrange("p (o n) -> p o n", o=C) for i in range(2))
        wf_big = bf_flat[:, 0:NW].rearrange("p (o n) -> p o n", o=C)
        wf_8 = bf_flat[:, NW:NW + NW // 2].bitcast(F8).rearrange("p (i o n) -> p i o n", i=2, o=C)
        wf_q = bf_flat[:, NW + NW // 2:2 * NW].bitcast(BF16).rearrange("p (o n) -> p o n", o=C)
        ctx_in = y[0:CT].rearrange("p a t c -> p (a t) c")
        k_ones = x_c[0:H].rearrange("p a t c -> p (a t c)").bitcast(F16)[:, 0:H * KP].rearrange(
            "p (h k) -> p h k", k=KP)
        spare = o_t[:].rearrange("p a g r -> p (a g r)")
        ctx_t = spare[:, 0:C * B * SK].rearrange("p (c k) -> p c k", c=C)
        keep = spare[:, C * B * SK:C * B * SK + ST * T * SK].rearrange("p (t k) -> p t k", k=SK)

        ps = stack.enter_context(nc.psum_tensor("ps", [P, 8, 512], F32))
        SC, OB, MX, GP = 0, SB, SB + 1, SB + 1 + MB
        wf_ps = ps[:, GP, 0:C * D // 2].bitcast(BF16)
        v_main = v_all[:, :, 0:H * LW].rearrange("p b (n e) -> p b n e", e=2)
        v_left = [v_all[32 * j:32 * j + L, :, H * LW:VB].rearrange("p b (g n) -> p b g n", g=G)
                  [:, :, :, 32 * j:32 * j + 32].rearrange("p b g (n e) -> p b g n e", e=2) for j in range(4)]

        ctx_in_s = sem("ctx_in_s")
        w_in = [sem(f"w_in{i}") for i in range(5)]
        mask_in_s = sem("mask_in_s")
        bias_in = sem("bias_in")
        x_a_in = [sem("x_a_in0"), sem("x_a_in1")]
        x_c_in = [sem("x_c_in0"), sem("x_c_in1")]
        pool_const = sem("pool_const")
        dve_const = sem("dve_const")
        one_made = sem("one_made")
        k_zeroed = sem("k_zeroed")
        k_ones_made = sem("k_ones_made")
        v_zeroed = sem("v_zeroed")
        v_ones = sem("v_ones")
        spread_made = sem("spread_made")
        q_ones = sem("q_ones")
        pro_pe = sem("pro_pe")
        pro_act = sem("pro_act")
        kt_done = sem("kt_done")
        khi_out = sem("khi_out")
        klo_out = sem("klo_out")
        v_done = sem("v_done")
        v_built = sem("v_built")
        neg_made = sem("neg_made")
        mask_dve = sem("mask_dve")
        mask_pool = sem("mask_pool")
        wf_dve = sem("wf_dve")
        wf_done = sem("wf_done")
        wf_out = sem("wf_out")
        k_sent = sem("k_sent")
        ones_sent = sem("ones_sent")
        k_built = sem("k_built")
        kmax_built = sem("kmax_built")
        kmax_in = [sem("kmax_in0"), sem("kmax_in1")]
        know_in = [sem("know_in0"), sem("know_in1")]
        vnow_in = [sem("vnow_in0"), sem("vnow_in1")]
        lna_dve = sem("lna_dve")
        lna_stats = sem("lna_stats")
        lna_pool = sem("lna_pool")
        xn_ready = sem("xn_ready")
        xt_done = sem("xt_done")
        xt_out = sem("xt_out")
        q_done = sem("q_done")
        qhi_out = sem("qhi_out")
        qlo_out = sem("qlo_out")
        q_sent = sem("q_sent")
        q_stacked = [[sem(f"q_stacked{i}{j}") for j in range(2)] for i in range(2)]
        max_done = sem("max_done")
        max_red = sem("max_red")
        mt_done = sem("mt_done")
        mt_out = sem("mt_out")
        mhalf_done = sem("mhalf_done")
        mhalf_out = sem("mhalf_out")
        mhalf_stacked = sem("mhalf_stacked")
        m_stacked = [sem("m_stacked0"), sem("m_stacked1")]
        sc_done = sem("sc_done")
        exp_done = sem("exp_done")
        pv_done = sem("pv_done")
        ot_out = sem("ot_out")
        a_in = [sem("a_in0"), sem("a_in1")]
        sums_sent = sem("sums_sent")
        sums_in = sem("sums_in")
        recip = sem("recip")
        rs_split = sem("rs_split")
        rs_sent = sem("rs_sent")
        rsrow_in = sem("rsrow_in")
        rs_spread = sem("rs_spread")
        at_ready = sem("at_ready")
        xbo_ready = sem("xbo_ready")
        wo_done = sem("wo_done")
        x1_ready = sem("x1_ready")
        lnc_dve = sem("lnc_dve")
        lnc_stats = sem("lnc_stats")
        lnc_pool = sem("lnc_pool")
        xq_ready = sem("xq_ready")
        xqt_done = sem("xqt_done")
        xqt_out = sem("xqt_out")
        x1bf_ready = sem("x1bf_ready")
        ff_done = sem("ff_done")
        ff_out = sem("ff_out")
        y_ready = sem("y_ready")
        y_bias = sem("y_bias")
        y_last = sem("y_last")
        last_stored = sem("last_stored")
        stored = [sem("stored0"), sem("stored1")]

        past_sp, past_pool, past_act, past_dve, past_pe = (
            sem(f"past_{e}") for e in ("sp", "pool", "act", "dve", "pe"))

        LAST = (B - 1, 1)

        block = stack.enter_context(nc.Block())

        @block.sync
        def _(sp):
            def load_x_a(k):
                if not first(k, 2):
                    sp.wait_ge(xn_ready, at(k, 1, -1))
                sp.sem_inc(past_sp, 1)
                sp.dma_start(x_a[:, k[1]], x_rows[bass.ds(at(k, 1), 1)].rearrange("s p t c -> p (s t) c")
                             ).then_inc(x_a_in[k[1]], 16)

            def send_q(k):
                sp.wait_ge(qhi_out, at(k, C, C))
                sp.wait_ge(qlo_out, at(k, C, C))
                for n, part in enumerate((q_hi, q_lo)):
                    sp.dma_start(q_dram[k[1], n].rearrange("(c p) r -> p c r", p=P), part[:]).then_inc(q_sent, 16)

            def stack_q(k, half):
                sp.wait_ge(q_sent, at(k, 32, 32))
                if not first(k, 2):
                    sp.sem_inc(past_sp, 1)
                    sp.wait_ge(sc_done, at(k, NC, (half - 3) * NC // 2))
                for n, part in enumerate((0, 0, 1)):
                    sp.dma_start(q_st[32 * n:32 * n + 32, k[1], 4 * half:4 * half + 4],
                                 q_dram[k[1], part].rearrange("(p d) r -> d p r", d=32)[:, 4 * half:4 * half + 4]
                                 ).then_inc(q_stacked[k[1]][half], 16)

            def stack_m(k):
                sp.wait_ge(mt_out, at(k, 1, 1))
                sp.dma_start(q_st[KM:KR, k[1]], m_t[:, None, :].to_broadcast([H, NP, R])).then_inc(m_stacked[k[1]], 16)

            def outputs(k, g):
                sp.wait_ge(ot_out, at(k, G, g + 1))
                if g == 0 and not first(k, 2):
                    sp.sem_inc(past_sp, 1)
                    sp.wait_ge(at_ready, at(k, C, -C))
                sp.dma_start(a_raw[64 * (g % 2):64 * (g % 2) + 64, k[1], g // 2], o_t[0:P:2, k[1], g]
                             ).then_inc(a_in[k[1]], 16)

            def sums_and_last_outputs(k):
                sp.wait_ge(ot_out, at(k, G, G))
                sp.dma_start(s_dram.rearrange("(g i r) -> i g r", i=4, r=R), o_t[1:P:32, k[1]]
                             ).then_inc(sums_sent, 16)
                outputs(k, G - 1)
                sp.wait_ge(sums_sent, at(k, 16, 16))
                if not first(k, 1):
                    sp.sem_inc(past_sp, 1)
                    sp.wait_ge(recip, at(k, 1))
                sp.dma_start(sums[:, :], s_dram.rearrange("(p w) -> p w", p=P)).then_inc(sums_in, 16)

            def send_reciprocals(k):
                sp.wait_ge(rs_split, at(k, 2, 2))
                sp.dma_start(r_dram.rearrange("i (p w) -> p i w", p=P), rs_16[:]).then_inc(rs_sent, 16)
                sp.wait_ge(rs_sent, at(k, 16, 16))
                if not first(k, 1):
                    sp.sem_inc(past_sp, 1)
                    sp.wait_ge(rs_spread, at(k, C))
                sp.dma_start(rs_row[:, :], r_dram.rearrange("i (h r) -> (i h) r", r=R)).then_inc(rsrow_in, 16)

            def keys_of(b):
                return k_all[:].rearrange("r p s b k -> r (p s) (b k)")[:, :, bass.ds(b * KP, KP)]

            def half_of(keys, half):
                return keys[:, NP * half:NP * half + NP]

            def k_max_for(b, half):
                sp.dma_start(half_of(k_max[:].rearrange("r p s k -> r (p s) k"), half), half_of(keys_of(b), half)
                             ).then_inc(kmax_in[half], 16)

            def k_now_for(b, half):
                sp.dma_start(half_of(k_now[:].rearrange("r p s k -> r (p s) k"), half), half_of(keys_of(b), half)
                             ).then_inc(know_in[half], 16)

            def v_now_for(b, half):
                W = VB // 4
                sp.dma_start(v_now[:].rearrange("p (m n) -> p m n", m=2)[:, :, W * half:W * half + W],
                             v_all[:].rearrange("p b (m n) -> p (b m) n", m=2)[:, bass.ds(b * 2, 2),
                                                                              W * half:W * half + W]
                             ).then_inc(vnow_in[half], 16)

            sp.dma_start(mask_in[:, :, :].rearrange("p (s t) k -> p s t k", s=ST), mask_rows
                         ).then_inc(mask_in_s, 16)
            sp.dma_start(w_raw[:, 0], wq.rearrange("(o p) n -> p o n", p=P)).then_inc(w_in[0], 16)
            load_x_a((0, 0))
            load_x_a((0, 1))
            sp.wait_ge(one_made, 1)
            sp.dma_start(q_st[KM - 1:KM].rearrange("c i p r -> c (i p) r"),
                         one_row[0:1, None, :].to_broadcast([1, 2 * NP, R])).then_inc(q_ones, 16)
            sp.dma_start(q_st[KM:KR, 0, 0:NP // 2], one_row[:, None, :].to_broadcast([H, NP // 2, R])
                         ).then_inc(q_ones, 16)
            sp.dma_start(bo_all[:, :], bass.AP(bo.tensor, 0, [[0, P], [1, D]])).then_inc(bias_in, 16)
            sp.dma_start(bf_all[:, :], bass.AP(bf.tensor, 0, [[0, P], [1, D]])).then_inc(bias_in, 16)

            sp.wait_ge(k_ones_made, 1)
            sp.wait_ge(k_zeroed, 2)
            sp.dma_start(k_max[KM:KR].rearrange("r p s k -> r (p s) k"), k_ones).then_inc(ones_sent, 16)
            for b in range(B):
                sp.dma_start(k_all[KM:KR, :, :, b].rearrange("r p s k -> r (p s) k"), k_ones).then_inc(ones_sent, 16)
            sp.wait_ge(khi_out, 2 * C)
            sp.wait_ge(klo_out, 2 * C)
            for n, part in enumerate((k_hi, k_lo)):
                sp.dma_start(k_dram[n].rearrange("(c p) k -> p c k", p=P),
                             part[:].rearrange("p c b k -> p c (b k)")).then_inc(k_sent, 16)
            sp.wait_ge(k_sent, 32)
            for s in range(2):
                for n, part in enumerate((0, 1, 0)):
                    row = 32 * n + DK * s
                    sp.dma_start(k_max[row:row + DK, :, s],
                                 k_dram[part].rearrange("(p s d) k -> s d p k", s=2, d=DK)[s][:, :, 0:KP]
                                 ).then_inc(kmax_built, 16)
            sp.wait_ge(neg_made, 1)
            sp.dma_start(k_max[KM - 1:KM].rearrange("r p s k -> r (p s) k"),
                         bass.AP(neg_row[:].tensor, 0, [[KP, 1], [0, NP * 2], [1, KP]])).then_inc(kmax_built, 16)
            stack_q((0, 0), 0)
            load_x_a((1, 0))
            stack_q((0, 0), 1)
            for s in range(2):
                for n, part in enumerate((0, 1, 0)):
                    row = 32 * n + DK * s
                    sp.dma_start(k_all[row:row + DK, :, s].rearrange("r p b k -> r p (b k)"),
                                 k_dram[part].rearrange("(p s d) k -> s d p k", s=2, d=DK)[s]).then_inc(k_built, 16)
            sp.dma_start(k_all[KM - 1:KM].rearrange("r p s b k -> r (p s b) k"),
                         bass.AP(neg_row[:].tensor, 0, [[KP, 1], [0, B * NP * 2], [1, KP]])).then_inc(k_built, 16)
            sp.wait_ge(k_built, 16 * 7)
            sp.wait_ge(ones_sent, 16 * (1 + B))
            k_now_for(0, 0)
            sp.wait_ge(v_built, 2 + 4)
            sp.wait_ge(v_ones, 5)
            v_now_for(0, 0)
            sp.wait_ge(q_ones, 32)
            sp.wait_ge(mhalf_out, 1)
            sp.dma_start(q_st[KM:KM + H // 2, 0, 0:NP // 2], m_t[0:H // 2, None, :].to_broadcast([H // 2, NP // 2, R])
                         ).then_inc(mhalf_stacked, 16)
            send_q((0, 1))
            stack_q((0, 1), 0)
            k_now_for(0, 1)
            v_now_for(0, 1)
            stack_q((0, 1), 1)
            sp.wait_ge(mt_out, 1)
            sp.dma_start(q_st[KM:KR, 0, NP // 2:NP], m_t[:, None, :].to_broadcast([H, NP // 2, R])
                         ).then_inc(m_stacked[0], 16)
            load_x_a((1, 1))

            def step(k, more=2, back=True):
                j, n, a = ahead(k, -1), ahead(k, 1), ahead(k, 2)
                if more > 1 and not first(k, 2):
                    load_x_a(a)
                if more > 0 and not first(k, 1):
                    stack_q(n, 1)
                if back and k[1] == 0:
                    sp.wait_ge(sc_done, at(k, NC))
                    sp.sem_inc(past_sp, 1)
                    k_now_for(k[0], 1)
                if back:
                    sums_and_last_outputs(j)
                if back and k[1] == 0:
                    sp.wait_ge(pv_done, at(k, G))
                    sp.sem_inc(past_sp, 1)
                    v_now_for(k[0], 1)
                outputs(k, 0)
                if back:
                    send_reciprocals(j)
                if more > 1 and k[1] == 0:
                    sp.wait_ge(max_done, at(n, NU, NU // 2))
                    sp.sem_inc(past_sp, 1)
                    k_max_for(a[0], 0)
                if more > 0 and k[1] == 1:
                    sp.wait_ge(sc_done, at(k, NC, NC // 2))
                    sp.sem_inc(past_sp, 1)
                    k_now_for(n[0], 0)
                if more > 1:
                    send_q(a)
                outputs(k, 1)
                if more > 0 and k[1] == 1:
                    sp.wait_ge(pv_done, at(k, G, G // 2))
                    sp.sem_inc(past_sp, 1)
                    v_now_for(n[0], 0)
                if more > 0:
                    stack_m(n)
                if more > 1:
                    stack_q(a, 0)
                if more > 1 and k[1] == 0:
                    sp.wait_ge(max_done, at(n, NU, NU))
                    sp.sem_inc(past_sp, 1)
                    k_max_for(a[0], 1)
                outputs(k, 2)

            step((0, 0), back=False)
            step((0, 1))
            with sp.Fori(1, B - 1) as h:
                step((h, 0))
                step((h, 1))
            step((B - 1, 0), more=1)
            step(LAST, more=0)
            sums_and_last_outputs(LAST)
            send_reciprocals(LAST)
            for u in range(C):
                sp.wait_ge(y_last, u + 1)
                sp.dma_start(out_rows[NB - 1, :, 2 * u:2 * u + 2], y[:, 1, 2 * u:2 * u + 2]).then_inc(last_stored, 16)
            sp.wait_ge(last_stored, 16 * C)

        @block.gpsimd
        def _(pool):
            pool.sem_inc(y_ready, 1)
            nc.gpsimd.memset(ident[:, :], 0.0).then_inc(pool_const, 1)
            nc.gpsimd.memset(half[:, :], -0.5).then_inc(pool_const, 1)
            pool.wait_ge(pool_const, 2)
            nc.gpsimd.affine_select(out=ident[:, :], in_=ident[:, :], compare_op=ALU.not_equal, fill=1.0,
                                    base=0, pattern=[[-1, P]], channel_multiplier=1).then_inc(pool_const, 1)
            nc.gpsimd.memset(one_row[:, :], 1.0).then_inc(one_made, 1)
            for keys in (k_max[:].rearrange("r p s k -> r (p s k)"), k_all[:].rearrange("r p s b k -> r (p s b k)")):
                nc.gpsimd.memset(keys.bitcast(F32), 0.0).then_inc(k_zeroed, 1)

            def ln_a(k):
                pool.wait_ge(lna_stats, at(k, 1, 1))
                nc.gpsimd.tensor_tensor(rs_a[:, 0], ve_a[:, 0], half[:, :], ALU.pow).then_inc(lna_pool, 1)
                pool.wait_ge(lna_pool, at(k, 3, 1))
                pool.wait_ge(mask_dve, 2)
                nc.gpsimd.tensor_tensor(rs_a[:, 1], rs_a[:, 0], row_keep[:, T * k[1]:T * k[1] + T], ALU.mult
                                        ).then_inc(lna_pool, 1)
                pool.wait_ge(lna_pool, at(k, 3, 2))
                nc.gpsimd.tensor_tensor(rs_a[:, 2], rs_a[:, 1], ve_a[:, 1], ALU.mult).then_inc(lna_pool, 1)
                pool.wait_ge(lna_pool, at(k, 3, 3))
                if not first(k, 1):
                    pool.wait_ge(xt_done, at(k, C))
                pool.sem_inc(past_pool, 1)
                for t in range(T):
                    last = nc.gpsimd.tensor_scalar(xn[:, t], x_a[:, k[1], t], rs_a[:, 1, t:t + 1],
                                                   rs_a[:, 2, t:t + 1], ALU.mult, ALU.add)
                last.then_inc(xn_ready, 1)

            def load_x_c(k):
                if not first(k, 2):
                    pool.wait_ge(xbo_ready, at(k, 1, -1))
                    pool.sem_inc(past_pool, 1)
                pool.dma_start(x_c[:, k[1]], x_rows[bass.ds(at(k, 1), 1)].rearrange("s p t c -> p (s t) c")
                               ).then_inc(x_c_in[k[1]], 16)

            def residual(k):
                pool.wait_ge(bias_in, 32)
                pool.wait_ge(x_c_in[k[1]], at((k[0], 0), 8, 16))
                if not first(k, 1):
                    pool.wait_ge(x1_ready, at(k, C))
                nc.gpsimd.tensor_tensor(x_bo[:], x_c[:, k[1]], bo_all[:, None, :].to_broadcast([P, T, D]),
                                        ALU.add).then_inc(xbo_ready, 1)

            def ln_c(k):
                pool.wait_ge(lnc_stats, at(k, 1, 1))
                if not first(k, 1):
                    pool.wait_ge(xq_ready, at(k, T))
                nc.gpsimd.tensor_tensor(rs_c[:, 0], ve_c[:, 0], half[:, :], ALU.pow).then_inc(lnc_pool, 1)
                pool.wait_ge(lnc_pool, at(k, 2, 1))
                nc.gpsimd.tensor_tensor(rs_c[:, 1], rs_c[:, 0], ve_c[:, 1], ALU.mult).then_inc(lnc_pool, 1)

            def add_bias(k):
                pool.wait_ge(x1_ready, at(k, C, C))
                if not first(k, 1):
                    pool.wait_ge(y_ready, at(k, 1, 1))
                nc.gpsimd.tensor_tensor(x1_bf[:], x1[:], bf_all[:, None, :].to_broadcast([P, T, D]), ALU.add
                                        ).then_inc(x1bf_ready, 1)

            def finish(k):
                pool.wait_ge(x1bf_ready, at(k, 1, 1))
                pool.wait_ge(ff_out, at(k, C, C))
                nc.gpsimd.tensor_tensor(y[:, k[1]], x1_bf[:], ff[:], ALU.add).then_inc(y_ready, 1)
                pool.wait_ge(y_ready, at(k, 1, 2))
                pool.sem_inc(past_pool, 1)
                pool.dma_start(out_rows[bass.ds(at(k, 1), 1)].rearrange("s p t c -> p (s t) c"), y[:, k[1]]
                               ).then_inc(stored[k[1]], 16)

            ln_a((0, 0))
            pool.wait_ge(mask_dve, 3)
            nc.gpsimd.partition_all_reduce(col_keep[:, :], col_part[:, :], P, RMAX).then_inc(mask_pool, 1)
            ln_a((0, 1))
            nc.gpsimd.memset(v_all[:, :, H * LW:VB], 0.0).then_inc(v_zeroed, 1)
            nc.gpsimd.memset(v_main[:, :, :, 1], 1.0 / RS).then_inc(v_ones, 1)
            pool.wait_ge(v_zeroed, 1)
            pool.wait_ge(v_ones, 1)
            for j in range(4):
                nc.gpsimd.memset(v_left[j][:, :, :, :, 1], 1.0 / RS).then_inc(v_ones, 1)
            pool.wait_ge(v_ones, 5)
            pool.wait_ge(mask_dve, 5)
            nc.gpsimd.partition_all_reduce(own_any[:, :], own_part[:, :], P, RMAX).then_inc(mask_pool, 1)
            nc.gpsimd.memset(spread[:], 0.0).then_inc(pool_const, 1)
            for part in range(2):
                pool.wait_ge(pool_const, 4 + part)
                to = spread[:].rearrange("p c (h d) -> p c h d", d=DK)
                nc.gpsimd.affine_select(out=to, in_=to, compare_op=ALU.not_equal, fill=1.0 / RS, base=-H * part,
                                        pattern=[[-8, C], [-1, 8], [0, DK]], channel_multiplier=1
                                        ).then_inc(spread_made if part else pool_const, 1)
            pool.wait_ge(ones_sent, 16 * (1 + B))

            def step(k, more=2, back=2):
                if more > 1:
                    ln_a(ahead(k, 2))
                load_x_c(k)
                if back > 1:
                    finish(ahead(k, -2))
                if back > 0:
                    residual(ahead(k, -1))
                    ln_c(ahead(k, -1))
                    add_bias(ahead(k, -1))
                if back > 1:
                    i = ahead(k, -2)
                    pool.wait_ge(stored[i[1]], at((i[0], 0), 8, 16))

            step((0, 0), back=0)
            step((0, 1), back=1)
            with pool.Fori(1, B - 1) as h:
                step((h, 0))
                step((h, 1))
            step((B - 1, 0), more=1)
            step(LAST, more=0)
            residual(LAST)
            ln_c(LAST)
            finish(ahead(LAST, -1))
            pool.wait_ge(stored[0], 16 * B)
            pool.wait_ge(stored[1], 16 * (B - 1))

        @block.scalar
        def _(act):
            act.dma_start(ctx_in, ctx.rearrange("b (u r) c -> r (b u) c", u=2)).then_inc(ctx_in_s, 16)
            act.dma_start(w_raw[:, 1], wk.rearrange("(o p) n -> p o n", p=P)).then_inc(w_in[1], 16)
            for i, w in ((2, wv), (3, wo)):
                act.dma_start(w_raw[:, i], w.rearrange("(o p) n -> p o n", p=P)).then_inc(w_in[i], 16)
            act.dma_start(wf_raw, wf.rearrange("(o p) n -> p o n", p=P)).then_inc(w_in[4], 16)

            def evacuate(n, dst, src):
                act.wait_ge(pro_pe, n)
                nc.scalar.activation(dst, src, ACT.Copy).then_inc(pro_act, 1)

            def weight_out(n, i, bank):
                evacuate(n, w_t[:, i].rearrange("p c n -> p (c n)"), ps[:, bank])

            for n in range(4):
                c, s = n // 2, n % 2
                evacuate(1 + n, ctx_t[:, c, s * 2 * SK:(s + 1) * 2 * SK], ps[:, 1 + n, 0:2 * SK])
            weight_out(5, 1, 0)
            weight_out(6, 0, 5)
            nc.scalar.activation(k_ones, ident[0:H, 0:H, None].to_broadcast([H, H, KP]), ACT.Copy
                                 ).then_inc(k_ones_made, 1)
            for n in range(2 * C):
                c, s = n // 2, n % 2
                act.wait_ge(kt_done, n + 1)
                nc.scalar.activation(k_hi[:, c, 2 * s:2 * s + 2, 0:SK],
                                     ps[:, n, 0:2 * SK].rearrange("p (b k) -> p b k", b=2), ACT.Copy
                                     ).then_inc(khi_out, 1)

            def x_transposed(k):
                for c in range(C):
                    act.wait_ge(xt_done, at(k, C, c + 1))
                    if not first(k, 1) and c == 0:
                        act.wait_ge(q_done, at(k, C))
                    nc.scalar.activation(xn_t[:, c], ps[:, GP + c], ACT.Copy).then_inc(xt_out, 1)

            def q_high(k, c):
                act.wait_ge(q_done, at(k, C, c + 1))
                if not first(k, 1) and c == 0:
                    act.wait_ge(q_sent, at(k, 32))
                nc.scalar.activation(q_hi[:, c], ps[:, GP + c], ACT.Copy).then_inc(qhi_out, 1)

            def max_transposed(k):
                act.wait_ge(mt_done, at(k, 1, 1))
                if not first(k, 1):
                    j = ahead(k, -1)
                    act.wait_ge(m_stacked[j[1]], at((j[0], 0), 8, 16))
                nc.scalar.activation(m_t[:, :], ps[0:H, MX + NU % MB], ACT.Copy).then_inc(mt_out, 1)

            def exps(k, n):
                g = n // CH
                if n % CH == 0 and (not first(k, 1) or g >= 2):
                    act.wait_ge(pv_done, at(k, G, g - 1))
                act.wait_ge(sc_done, at(k, NC, n + 1))
                nc.scalar.activation(p_t[:, g % 2, n % CH], ps[:, SC + n % SB], ACT.Exp, scale=DK ** -0.5
                                     ).then_inc(exp_done, 1)

            def heads_out(k, g):
                act.wait_ge(pv_done, at(k, G, g + 1))
                if g == 0 and not first(k, 2):
                    act.wait_ge(a_in[k[1]], at((k[0], 0), 8 * G))
                    act.wait_ge(sums_sent, at(k, 16, -16))
                nc.scalar.activation(o_t[:, k[1], g], ps[:, OB], ACT.Copy).then_inc(ot_out, 1)

            def quantised_transposed(k):
                for c in range(C):
                    act.wait_ge(xqt_done, at(k, C, c + 1))
                    nc.scalar.activation(xq_t[:, c], ps[:, GP + c], ACT.Copy).then_inc(xqt_out, 1)

            def layer_out(k):
                for u in range(C):
                    act.wait_ge(ff_done, at(k, C, u + 1))
                    if not first(k, 1) and u == 0:
                        act.wait_ge(y_ready, at(k, 1, 1))
                    nc.scalar.activation(ff[:, 2 * u:2 * u + 2].rearrange("p t c -> p (t c)"), ps[:, GP + u],
                                         ACT.Copy).then_inc(ff_out, 1)

            def quantise(k, t):
                if t == 0:
                    act.wait_ge(lnc_pool, at(k, 2, 2))
                    act.sem_inc(past_act, 1)
                nc.scalar.activation(xq[:, t], x1[:, t], ACT.Identity, bias=rs_c[:, 1, t:t + 1],
                                     scale=rs_c[:, 0, t:t + 1], saturate=False).then_inc(xq_ready, 1)

            x_transposed((0, 0))
            weight_out(7, 2, 4)
            weight_out(8, 3, 5)
            for c in range(C):
                q_high((0, 0), c)
            act.wait_ge(qlo_out, C)
            for n, part in enumerate((q_hi, q_lo)):
                act.dma_start(q_dram[0, n].rearrange("(c p) r -> p c r", p=P), part[:]).then_inc(q_sent, 16)
            act.wait_ge(v_done, 1)
            for s in range(2):
                nc.scalar.activation(v_main[:, 2 * s:2 * s + 2, :, 0], ps[:, s].rearrange("p (b n) -> p b n", b=2),
                                     ACT.Copy).then_inc(v_built, 1)
            act.wait_ge(v_done, 2)
            act.wait_ge(v_zeroed, 1)
            for j in range(4):
                nc.scalar.activation(v_left[j][:, :, :, :, 0],
                                     ps[32 * j:32 * j + L, 2, 0:D].rearrange("p (b g d) -> p b g d", b=B, g=G),
                                     ACT.Copy).then_inc(v_built, 1)
            x_transposed((0, 1))
            for c in range(C):
                q_high((0, 1), c)
            act.wait_ge(mhalf_done, 1)
            nc.scalar.activation(m_t[0:H // 2, :], ps[0:H // 2, SC], ACT.Copy).then_inc(mhalf_out, 1)

            def step(k, more=2, back=2):
                i, j, n, a = ahead(k, -2), ahead(k, -1), ahead(k, 1), ahead(k, 2)
                zx = ZX if back > 1 else ZX_0
                for z in range(NC):
                    exps(k, z)
                    if z == 2 and back == 1 and first(k, 2):
                        act.wait_ge(wf_done, 1)
                        nc.scalar.activation(wf_t[:].rearrange("p c n -> p (c n)"), wf_ps, ACT.Copy
                                             ).then_inc(wf_out, 1)
                    if z == 1 and back == 0:
                        act.wait_ge(mhalf_stacked, 16)
                        max_transposed(k)
                    if z == 2 and back > 0:
                        heads_out(j, G - 1)
                    if z in (0, 1, 2, 3) and back > 1:
                        quantise(i, z)
                    if z == 5 and more > 0 and back > 1:
                        quantised_transposed(i)
                    if z == 7 and more > 0 and back > 1:
                        layer_out(i)
                    if z % CH == 2 and z > CH and more > 0:
                        heads_out(k, z // CH - 1)
                    if z == zx and more > 1:
                        x_transposed(a)
                    if z in (zx + 2, zx + 3) and more > 1:
                        q_high(a, z - zx - 2)
                    if z == MZ and more > 0:
                        max_transposed(n)

            step((0, 0), back=0)
            step((0, 1), back=1)
            with act.Fori(1, B - 1) as h:
                step((h, 0))
                step((h, 1))
            step((B - 1, 0), more=1)
            step(LAST, more=0)
            act.wait_ge(ff_done, C * (NB - 2))
            for t in range(T):
                quantise(ahead(LAST, -1), t)
            quantised_transposed(ahead(LAST, -1))
            layer_out(ahead(LAST, -1))
            for t in range(T // 2):
                quantise(LAST, t)
            quantised_transposed(LAST)
            layer_out(LAST)

        @block.vector
        def _(dve):
            def row_stats(src, stats, done, t):
                nc.vector.bn_stats(stats[:, t], src[:, t]).then_inc(done, 1)

            def row_moments(k, stats, mv, done):
                for t in range(T):
                    dve.wait_ge(done, at(k, 2 * T, t + 1))
                    dve.sem_inc(past_dve, 1)
                    nc.vector.bn_aggr(mv[:, t], stats[:, t]).then_inc(done, 1)
                dve.wait_ge(done, at(k, 2 * T, 2 * T))

            def stats_a(k, t):
                if t == 0:
                    dve.wait_ge(x_a_in[k[1]], at((k[0], 0), 8, 16))
                row_stats(x_a[:, k[1]], st_a, lna_dve, t)

            def moments_a(k):
                row_moments(k, st_a, mv_a, lna_dve)
                if not first(k, 1):
                    dve.wait_ge(lna_pool, at(k, 3))
                nc.vector.tensor_scalar(ve_a[:, 0], mv_a[:, :, 1], EPS, None, ALU.add)
                nc.vector.tensor_scalar(ve_a[:, 1], mv_a[:, :, 0], -1.0, None, ALU.mult
                                        ).then_inc(lna_stats, 1)

            def q_low(k, c):
                dve.wait_ge(qhi_out, at(k, C, c + 1))
                if not first(k, 1) and c == 0:
                    dve.wait_ge(q_sent, at(k, 32))
                nc.vector.tensor_tensor(q_lo[:, c], ps[:, GP + c], q_hi[:, c], ALU.subtract
                                        ).then_inc(qlo_out, 1)

            def maxima(k, u):
                if u == 0 and not first(k, 1):
                    dve.wait_ge(mt_done, at(k, 1))
                p, t = u // T, u % T
                dve.wait_ge(max_done, at(k, NU, u + 1))
                nc.vector.tensor_reduce(m_neg[:, t, 2 * p:2 * p + 2],
                                        ps[:, MX + u % MB, 0:2 * SK].rearrange("p (s k) -> p s k", s=2),
                                        X, ALU.max, negate=True).then_inc(max_red, 1)

            def reciprocals(k):
                dve.wait_ge(sums_in, at(k, 16, 16))
                nc.vector.reciprocal(rsum[:, :], sums[:, :]).then_inc(recip, 1)
                dve.wait_ge(recip, at(k, 1, 1))
                if not first(k, 1):
                    dve.wait_ge(rs_sent, at(k, 16))
                nc.vector.tensor_copy(rs_16[:, 0], rsum[:, :]).then_inc(rs_split, 1)
                dve.wait_ge(rs_split, at(k, 2, 1))
                nc.vector.tensor_tensor(rs_16[:, 1], rsum[:, :], rs_16[:, 0], ALU.subtract).then_inc(rs_split, 1)

            def normalise(k):
                dve.wait_ge(a_in[k[1]], at((k[0], 0), 8 * G, 16 * G))
                if not first(k, 1):
                    dve.wait_ge(wo_done, at(k, C))
                for c in range(C):
                    dve.wait_ge(rs_spread, at(k, C, c + 1))
                    nc.vector.tensor_tensor(a_t[:, c], ps[:, GP + c], a_raw[:, k[1], c], ALU.mult
                                            ).then_inc(at_ready, 1)

            def add_residual(k, u):
                dve.wait_ge(xbo_ready, at(k, 1, 1))
                dve.wait_ge(wo_done, at(k, C, u + 1))
                if u == 0 and not first(k, 1):
                    dve.wait_ge(x1bf_ready, at(k, 1))
                nc.vector.tensor_tensor(x1[:, 2 * u:2 * u + 2].rearrange("p t c -> p (t c)"), ps[:, GP + u],
                                        x_bo[:, 2 * u:2 * u + 2].rearrange("p t c -> p (t c)"), ALU.add
                                        ).then_inc(x1_ready, 1)

            def stats_c(k, t):
                if t % 2 == 0:
                    dve.wait_ge(x1_ready, at(k, C, t // 2 + 1))
                    dve.sem_inc(past_dve, 1)
                row_stats(x1, st_c, lnc_dve, t)

            def moments_c(k):
                row_moments(k, st_c, mv_c, lnc_dve)
                if not first(k, 1):
                    dve.wait_ge(lnc_pool, at(k, 2))
                nc.vector.tensor_scalar(ve_c[:, 0], mv_c[:, :, 1], EPS, None, ALU.add)
                nc.vector.tensor_scalar(ve_c[:, 1], mv_c[:, :, 0], -1.0, None, ALU.mult
                                        ).then_inc(lnc_stats, 1)

            def quantise_weight():
                dve.wait_ge(w_in[4], 16)
                nc.vector.tensor_scalar(wf_small, wf_raw, 240.0, -240.0, ALU.min, ALU.max)
                nc.vector.tensor_scalar(wf_big, wf_raw, 448.0, -448.0, ALU.min, ALU.max).then_inc(wf_dve, 1)
                dve.wait_ge(wf_dve, 1)
                nc.vector.tensor_scalar(wf_8[:, 0], wf_small, 1.0, None, ALU.mult, saturate=False)
                nc.vector.tensor_scalar(wf_8[:, 1], wf_big, 0.5, None, ALU.mult, saturate=False
                                        ).then_inc(wf_dve, 1)
                dve.wait_ge(wf_dve, 2)
                nc.vector.tensor_scalar(wf_big, wf_8[:, 1], 2.0, None, ALU.mult).then_inc(wf_dve, 1)
                dve.wait_ge(wf_dve, 3)
                nc.vector.tensor_tensor(wf_big, wf_big, wf_8[:, 0], ALU.subtract)
                nc.vector.tensor_tensor(wf_small, wf_raw, wf_raw, ALU.mult).then_inc(wf_dve, 1)
                dve.wait_ge(wf_dve, 4)
                nc.vector.tensor_scalar(wf_small, wf_small, 256.0, None, ALU.is_ge).then_inc(wf_dve, 1)
                dve.wait_ge(wf_dve, 5)
                nc.vector.tensor_tensor(wf_small, wf_small, wf_big, ALU.mult).then_inc(wf_dve, 1)
                dve.wait_ge(wf_dve, 6)
                nc.vector.tensor_tensor(wf_q, wf_8[:, 0], wf_small, ALU.add).then_inc(wf_dve, 1)

            nc.vector.memset(k_hi[:, :, :, SK:KP], 0.0)
            nc.vector.memset(k_lo[:, :, :, SK:KP], 0.0)
            nc.vector.memset(mask_own[:, :, SK:KP], 0.0)
            dve.wait_ge(mask_in_s, 16)
            nc.vector.tensor_copy(keep, mask_in[:]).then_inc(mask_dve, 1)
            dve.wait_ge(mask_dve, 1)
            nc.vector.reduce_max(row_keep[:, :], keep, X).then_inc(mask_dve, 1)
            for t in range(T):
                stats_a((0, 0), t)
            moments_a((0, 0))
            nc.vector.reduce_max(col_part[:, :], keep.rearrange("p t k -> p k t"), X).then_inc(mask_dve, 1)
            dve.wait_ge(pool_const, 3)
            nc.vector.tensor_copy(ident16[:, :], ident[:, :]).then_inc(dve_const, 1)
            nc.vector.tensor_copy(identb[:, :], ident[:, :]).then_inc(dve_const, 1)
            nc.vector.tensor_scalar(ident8[:, :], ident[:, :], 1.0, None, ALU.mult, saturate=False
                                    ).then_inc(dve_const, 1)
            for t in range(T):
                stats_a((0, 1), t)
            moments_a((0, 1))
            for n in range(2 * C):
                c, s = n // 2, n % 2
                hi, lo = (part[:, c, 2 * s:2 * s + 2, 0:SK] for part in (k_hi, k_lo))
                dve.wait_ge(khi_out, n + 1)
                nc.vector.tensor_tensor(lo, ps[:, n, 0:2 * SK].rearrange("p (b k) -> p b k", b=2), hi, ALU.subtract
                                        ).then_inc(klo_out, 1)
            dve.wait_ge(mask_pool, 1)
            nc.vector.memset(neg_row[:, SK:KP], NEG)
            nc.vector.tensor_scalar(neg_row[:, 0:SK], col_keep[0:1, :], -NEG, NEG, ALU.mult, ALU.add
                                    ).then_inc(neg_made, 1)
            nc.vector.tensor_tensor(keep, keep, col_keep[:, None, :].to_broadcast([P, ST * T, SK]),
                                    ALU.subtract).then_inc(mask_dve, 1)
            dve.wait_ge(mask_dve, 4)
            nc.vector.tensor_reduce(own_part[:, :], keep, XY, ALU.min, negate=True).then_inc(mask_dve, 1)
            nc.vector.tensor_scalar(mask_own[:, :, 0:SK], keep, -NEG, None, ALU.mult).then_inc(mask_dve, 1)
            for c in range(C):
                q_low((0, 0), c)
            dve.wait_ge(mask_pool, 2)
            nc.vector.tensor_copy(own_flag[:, :], own_any[0:1, :]).then_inc(mask_dve, 1)
            quantise_weight()
            for c in range(C):
                for u in range(8 * c, 8 * c + 8):
                    maxima((0, 0), u)
                q_low((0, 1), c)
            for u in range(8 * C, EARLY):
                maxima((0, 0), u)

            def step(k, more=2, back=2):
                j, n, a = ahead(k, -1), ahead(k, 1), ahead(k, 2)
                zx = ZX if back > 1 else ZX_0
                for z in range(NC):
                    if z == 0 and not back:
                        for u in range(EARLY, NU):
                            maxima(k, u)
                    for u in units(WITH if back > 1 else WITH_0, z) if more > 0 else ():
                        maxima(n, u)
                    zs = zx - 8 if back > 1 else 0
                    if zs <= z < zs + T and more > 1:
                        stats_a(a, z - zs)
                        if z == zs + T - 1:
                            moments_a(a)
                    if z == 8 and back:
                        reciprocals(j)
                    if z in (zx + 2, zx + 3) and more > 1:
                        q_low(a, z - zx - 2)
                    if z == ZC and back and more > 0:
                        normalise(j)
                    if z in (ZC + 1, ZC + 2) and back and more > 0:
                        u = z - ZC - 1
                        add_residual(j, u)
                        for t in (2 * u, 2 * u + 1):
                            stats_c(j, t)
                    if z == ZC + 3 and back and more > 0:
                        moments_c(j)

            step((0, 0), back=0)
            step((0, 1), back=1)
            with dve.Fori(1, B - 1) as h:
                step((h, 0))
                step((h, 1))
            step((B - 1, 0), more=1)
            def heads_out(g):
                dve.wait_ge(pv_done, G * (NB - 1) + g + 1)
                if g == 0:
                    dve.wait_ge(a_in[1], 16 * G * (B - 1))
                    dve.wait_ge(sums_sent, 16 * (NB - 2))
                nc.vector.tensor_copy(o_t[:, 1, g], ps[:, OB]).then_inc(ot_out, 1)

            for c in range(C):
                dve.wait_ge(xqt_done, C * (NB - 3) + c + 1)
                nc.vector.tensor_copy(xq_t[:, c], ps[:, GP + c]).then_inc(xqt_out, 1)
            for u in range(C):
                dve.wait_ge(ff_done, C * (NB - 3) + u + 1)
                if u == 0:
                    dve.wait_ge(y_ready, NB - 3 + 1)
                nc.vector.tensor_copy(ff[:, 2 * u:2 * u + 2].rearrange("p t c -> p (t c)"), ps[:, GP + u]
                                      ).then_inc(ff_out, 1)
            heads_out(0)
            reciprocals(ahead(LAST, -1))
            for g in range(1, G):
                heads_out(g)
            for k in (ahead(LAST, -1), LAST):
                normalise(k)
                for u in range(C):
                    if k == LAST and u == 0:
                        dve.wait_ge(xq_ready, T * (NB - 1))
                    add_residual(k, u)
                    for t in (2 * u, 2 * u + 1):
                        stats_c(k, t)
                    if k != LAST and u == 0:
                        reciprocals(LAST)
                moments_c(k)
            dve.wait_ge(bias_in, 32)
            dve.wait_ge(lnc_pool, 2 * NB)
            dve.wait_ge(xqt_done, C * (NB - 1))
            for t in range(T // 2, T):
                nc.vector.tensor_scalar(xq[:, t], x1[:, t], rs_c[:, 0, t:t + 1], rs_c[:, 1, t:t + 1], ALU.mult, ALU.add,
                                        saturate=False).then_inc(xq_ready, 1)
            dve.wait_ge(stored[1], 16 * (B - 1))
            for u in range(C):
                nc.vector.tensor_tensor(y[:, 1, 2 * u:2 * u + 2], x1[:, 2 * u:2 * u + 2],
                                        bf_all[:, None, :].to_broadcast([P, T // C, D]), ALU.add).then_inc(y_bias, 1)
            for u in range(C):
                dve.wait_ge(y_bias, u + 1)
                dve.wait_ge(ff_out, C * (NB - 1) + u + 1)
                nc.vector.tensor_tensor(y[:, 1, 2 * u:2 * u + 2], y[:, 1, 2 * u:2 * u + 2], ff[:, 2 * u:2 * u + 2],
                                        ALU.add).then_inc(y_last, 1)

        @block.tensor
        def _(pe):
            pe.wait_ge(pool_const, 3)

            def keep_warm(n, bank):
                for _ in range(n):
                    nc.tensor.matmul(ps[:, bank, 0:P], ident[:, :], ident[:, :], start=True, stop=True)

            keep_warm(WARM_IN, GP + 1)

            def transpose_weight(i, bank):
                pe.wait_ge(w_in[i], 16)
                for c in range(C):
                    for o in range(C):
                        last = nc.tensor.transpose(ps[:, bank, c * D + o * P:c * D + o * P + P],
                                                   w_raw[:, i, o, c * P:c * P + P], ident[:, :])
                last.then_inc(pro_pe, 1)

            pe.wait_ge(ctx_in_s, 16)
            for n in range(4):
                c, s = n // 2, n % 2
                for t in range(4):
                    last = nc.tensor.transpose(ps[:, 1 + n, t * CT:(t + 1) * CT],
                                               ctx_in[:, 4 * s + t, c * P:c * P + P], ident[0:CT, 0:CT])
                last.then_inc(pro_pe, 1)
            transpose_weight(1, 0)
            transpose_weight(0, 5)

            def transpose_x(k):
                pe.wait_ge(xn_ready, at(k, 1, 1))
                if not first(k, 4):
                    pe.wait_ge(ff_out, at(k, C, -3 * C))
                elif not first(k, 3):
                    pe.wait_ge(wf_out, 1)
                elif not first(k, 1):
                    pe.wait_ge(qlo_out, at(k, C))
                for c in range(C):
                    for t in range(T):
                        last = nc.tensor.transpose(ps[:, GP + c, t * P:t * P + P],
                                                   xn[:, t, c * P:c * P + P], ident[:, :])
                    last.then_inc(xt_done, 1)

            def project_q(k, c, parts=(0, 1)):
                if c == 0 and 0 in parts:
                    pe.wait_ge(xt_out, at(k, C, C))
                if c == 0 and first(k, 1):
                    pe.wait_ge(pro_act, 6)
                for i in parts:
                    last = nc.tensor.matmul(ps[:, GP + c], w_t[:, 0, i, c * P:c * P + P], xn_t[:, i],
                                            start=i == 0, stop=i == C - 1)
                if C - 1 in parts:
                    last.then_inc(q_done, 1)

            def transpose_m(k):
                pe.wait_ge(max_red, at(k, T * NP, T * NP))
                for t in range(T):
                    last = nc.tensor.transpose(ps[0:H, MX + NU % MB, t * P:t * P + P], m_neg[:, t], ident[:, :])
                last.then_inc(mt_done, 1)

            def write_out(own):

                def row_scores(k, u):
                    p, t = u // T, u % T
                    if u % (NU // 2) == 0:
                        half = u // (NU // 2)
                        pe.wait_ge(q_stacked[k[1]][half], at((k[0], 0), 24, 48))
                        if first(k, 1):
                            pe.wait_ge(q_ones, 32)
                            pe.wait_ge(ones_sent, 16 * (1 + B))
                            pe.wait_ge(kmax_built, 16 * 7)
                        elif not first(k, 2):
                            pe.wait_ge(kmax_in[half], at((k[0], 0), 8))
                    if not first(k, 1) and u == NU % MB:
                        pe.wait_ge(mt_out, at(k, 1))
                    elif not first(k, 1) and u < MB:
                        pe.wait_ge(max_red, at(k, NU, u - 1))
                    elif u >= MB:
                        pe.wait_ge(max_red, at(k, NU, u - MB + 1))
                    dst = ps[:, MX + u % MB, 0:2 * SK]
                    last = nc.tensor.matmul(dst, q_st[0:KM, k[1], p, t * P:t * P + P],
                                            k_max[0:KM, p, :, 0:SK], start=True, stop=not own)
                    if own:
                        last = nc.tensor.matmul(
                            dst, ident16[:, :],
                            mask_own[:, T * k[1] + t, None, 0:SK].to_broadcast([P, 2, SK]),
                            start=False, stop=True)
                    last.then_inc(max_done, 1)

                def scores(k, n):
                    g, c = n // CH, n % CH
                    if n == 0 and first(k, 1):
                        pe.wait_ge(v_built, 2 + 4)
                    if n == 0 and first(k, 1):
                        pe.wait_ge(mhalf_stacked, 16)
                    if n == (NC // 2 if first(k, 1) else 0):
                        pe.wait_ge(m_stacked[k[1]], at((k[0], 0), 8, 16))
                    if n % (NC // 2) == 0:
                        pe.wait_ge(know_in[n // (NC // 2)], at((k[0], 0), 8, 16))
                    if not first(k, 1) or n >= SB:
                        pe.wait_ge(exp_done, at(k, NC, n - SB + 1))
                    bank = ps[:, SC + n % SB]
                    heads = [(c, 0, P, bank)] if c < 4 else [
                        (j, P, KP, ps[32 * j:32 * j + LW, SC + n % SB]) for j in range(4)]
                    for j, lo, hi, dst in heads:
                        last = nc.tensor.matmul(dst, k_now[:, 2 * g + j // 2, j % 2, lo:hi],
                                                q_st[:, k[1], 2 * g + j // 2], start=True, stop=not own)
                        if own:
                            for t in range(T):
                                last = nc.tensor.matmul(dst[:, t * P:t * P + P],
                                                        mask_own[:, T * k[1] + t, lo:hi], ident16[:, :],
                                                        start=False, stop=t == T - 1)
                    last.then_inc(sc_done, 1)

                def values(k, n):
                    g, c = n // CH, n % CH
                    if c == 0:
                        if not first(k, 1) or g > 0:
                            pe.wait_ge(ot_out, at(k, G, g))
                        if g % 2 == 0:
                            pe.wait_ge(vnow_in[g // 2], at((k[0], 0), 8, 16))
                    pe.wait_ge(exp_done, at(k, NC, n + 1))
                    if c < 4:
                        h = 4 * g + c
                        nc.tensor.matmul(ps[32 * c:32 * c + LW, OB], v_now[:, h * LW:(h + 1) * LW],
                                         p_t[:, g % 2, c], start=True, stop=False)
                    else:
                        nc.tensor.matmul(ps[:, OB], v_now[:, H * LW + g * P:H * LW + (g + 1) * P],
                                         p_t[:, g % 2, c], start=False, stop=True).then_inc(pv_done, 1)

                def spread_reciprocals(k, emptied, count):
                    if first(k, 1):
                        pe.wait_ge(spread_made, 1)
                    pe.wait_ge(rsrow_in, at(k, 16, 16))
                    pe.wait_ge(emptied, count)
                    for c in range(C):
                        nc.tensor.matmul(ps[:, GP + c], spread[:, c], rs_row[:, :], start=True, stop=True
                                         ).then_inc(rs_spread, 1)

                def output(k, u):
                    if u == 0:
                        pe.wait_ge(at_ready, at(k, C, C))
                    for t in (2 * u, 2 * u + 1):
                        for c in range(C):
                            last = nc.tensor.matmul(ps[:, GP + u, (t % 2) * D:(t % 2 + 1) * D],
                                                    a_t[:, c, t * P:t * P + P], w_t[:, 3, c, :],
                                                    start=c == 0, stop=c == C - 1)
                    last.then_inc(wo_done, 1)

                def transpose_xq(k):
                    pe.wait_ge(xq_ready, at(k, T, T))
                    pe.sem_inc(past_pe, 1)
                    for c in range(C):
                        for t in range(T):
                            last = nc.tensor.matmul(ps[:, GP + c, t * P:t * P + P], xq[:, t, c * P:c * P + P],
                                                    ident8[:, :], start=True, stop=True)
                        last.then_inc(xqt_done, 1)

                def layer(k):
                    pe.wait_ge(xqt_out, at(k, C, C))
                    for u in range(C):
                        for t in (2 * u, 2 * u + 1):
                            for c in range(C):
                                last = nc.tensor.matmul(ps[:, GP + u, (t % 2) * D:(t % 2 + 1) * D],
                                                        xq_t[:, c, t * P:t * P + P], wf_t[:, c, :],
                                                        start=c == 0, stop=c == C - 1)
                        last.then_inc(ff_done, 1)

                def step(k, more=2, back=2):
                    i, j, n, a = ahead(k, -2), ahead(k, -1), ahead(k, 1), ahead(k, 2)
                    zx = ZX if back > 1 else ZX_0
                    for z in range(NC):
                        scores(k, z)
                        if z == 0 and back == 0:
                            for u in range(EARLY, NU):
                                row_scores(k, u)
                        if z == 1 and back == 0:
                            transpose_m(k)

                        def search(part):
                            for u in units(WITH if back > 1 else WITH_0, z, part, 3) if more > 0 else ():
                                row_scores(n, u)

                        search(0)
                        if z == 5 and back > 1:
                            transpose_xq(i)
                        if z == 7 and back > 1:
                            layer(i)
                        if z == zx and more > 1:
                            transpose_x(a)
                        if z in (zx + 2, zx + 3) and more > 1:
                            project_q(a, z - zx - 2, (0,))
                        search(1)
                        if z in (zx + 2, zx + 3) and more > 1:
                            project_q(a, z - zx - 2, (1,))
                        search(2)
                        if more > 0 and z == MZ:
                            transpose_m(n)
                        if z == ZC and back > 0 and more > 0:
                            if more > 1:
                                spread_reciprocals(j, qlo_out, at(a, C, C))
                            else:
                                spread_reciprocals(j, ff_out, at(j, C))
                        if z in (ZC + 1, ZC + 2) and back > 0 and more > 0:
                            output(j, z - ZC - 1)
                        if z == 2 and back == 1 and first(k, 2):
                            pe.wait_ge(wf_dve, 7)
                            pe.wait_ge(qlo_out, at(n, C, C))
                            for c in range(C):
                                for o in range(C):
                                    last = nc.tensor.transpose(wf_ps[:, c * D + o * P:c * D + o * P + P],
                                                               wf_q[:, o, c * P:c * P + P], identb[:, :])
                            last.then_inc(wf_done, 1)
                        due = ((z - LAG,), (z - LAG,), (z - LAG,), (), (z - LAG - 1, z - LAG))[z % CH]
                        if more == 0 and z > LAG:
                            due = ((z - LAG - 2, z - LAG - 1, z - LAG), (z - LAG,), (z - LAG,), (), ())[z % CH]
                        for v in due:
                            if v >= 0:
                                values(k, v)
                            elif back > 0:
                                values(j, NC + v)

                for c in range(C):
                    project_q((0, 1), c)
                    for u in range(8 * c, 8 * c + 8):
                        row_scores((0, 0), u)
                pe.wait_ge(max_red, NU // 2)
                pe.wait_ge(v_built, 2 + 4)
                for t in range(T):
                    last = nc.tensor.transpose(ps[0:H // 2, SC, t * P:t * P + P], m_neg[:, t, 0:H // 2], ident[:, :])
                last.then_inc(mhalf_done, 1)
                for u in range(8 * C, EARLY):
                    row_scores((0, 0), u)
                step((0, 0), back=0)
                step((0, 1), back=1)
                with pe.Fori(1, B - 1) as h:
                    step((h, 0))
                    step((h, 1))
                step((B - 1, 0), more=1)
                step(LAST, more=0)
                for z in range(NC - CH, NC):
                    values(LAST, z)
                for k, emptied, count in ((ahead(LAST, -1), ff_out, C * (NB - 2)), (LAST, x1_ready, C * (NB - 1))):
                    spread_reciprocals(k, emptied, count)
                    for u in range(C):
                        output(k, u)
                    if k != LAST:
                        pe.wait_ge(exp_done, NC * NB)
                        keep_warm(WARM_OUT, SC)
                pe.wait_ge(x1_ready, C * NB)
                for k in (ahead(LAST, -1), LAST):
                    if k == LAST:
                        pe.wait_ge(ff_out, C * (NB - 1))
                    transpose_xq(k)
                    layer(k)

            pe.wait_ge(pro_act, 5)
            for n in range(2 * C):
                c, s = n // 2, n % 2
                for i in range(C):
                    last = nc.tensor.matmul(ps[:, n, 0:2 * SK], w_t[:, 1, i, c * P:c * P + P],
                                            ctx_t[:, i, s * 2 * SK:(s + 1) * 2 * SK], start=i == 0, stop=i == C - 1)
                last.then_inc(kt_done, 1)
            transpose_x((0, 0))
            transpose_weight(2, 4)
            pe.wait_ge(pro_act, 6)
            transpose_weight(3, 5)
            for c in range(C):
                project_q((0, 0), c)
            pe.wait_ge(pro_act, 7)
            pe.wait_ge(klo_out, 3)
            for b in range(B):
                for i in range(C):
                    last = nc.tensor.matmul(ps[:, b // 2, (b % 2) * D:(b % 2 + 1) * D],
                                            ctx_t[:, i, b * SK:b * SK + P], w_t[:, 2, i, :],
                                            start=i == 0, stop=i == C - 1)
            last.then_inc(v_done, 1)
            for b in range(B):
                for j in range(4):
                    for i in range(C):
                        wv_j = w_t[:, 2, i, :].rearrange("p (g j d) -> p g j d", g=G, j=4)[:, :, j]
                        last = nc.tensor.matmul(ps[32 * j:32 * j + L, 2, b * G * DK:(b + 1) * G * DK],
                                                ctx_t[:, i, b * SK + P:(b + 1) * SK], wv_j,
                                                start=i == 0, stop=i == C - 1)
            last.then_inc(v_done, 1)
            transpose_x((0, 1))
            pe.wait_ge(dve_const, 3)
            pe.wait_ge(pro_act, 8)
            pe.wait_ge(klo_out, 4)
            pe.wait_ge(mask_dve, 7)
            differs = nc.tensor.value_load(own_flag[0:1, 0:1])
            with pe.If(differs > 0):
                write_out(True)
            with pe.Else():
                write_out(False)


_OUT = ((4, 1024, 256), "float32")
_INS = ["x", "ctx_1024", "mask_1x1xSxS2_bk0", "L0_xattn_Wq", "L0_xattn_Wk", "L0_xattn_Wv", "L0_xattn_Wo",
        "L0_xattn_bo", "L0_ffn_weight", "L0_ffn_bias"]


def kernel(**inputs):
    import numpy as _np
    import concourse.bacc as _bacc
    from concourse import mybir as _mybir
    from concourse.bass_utils import run_bass_kernel_spmd as _run

    nc = _bacc.Bacc("TRN2", target_bir_lowering=False, num_devices=1)
    arrays, args = {}, []
    for name in _INS:
        a = _np.ascontiguousarray(inputs[name])
        arrays[f"in_{name}_dram"] = a
        args.append(nc.dram_tensor(f"in_{name}_dram", a.shape, _mybir.dt.from_np(a.dtype), kind="ExternalInput").ap())
    dt = _mybir.dt.from_np(_np.dtype(_OUT[1]))
    args.append(nc.dram_tensor("out_dram", _OUT[0], dt, kind="ExternalOutput").ap())
    xattn_ffn(nc, *args)
    r = _run(nc, [arrays], core_ids=[0])
    return r.results[0]["out_dram"]
```
